# Optimizing a Trainium2 kernel written in Bass

```python
import numpy as np
import jax
import jax.numpy as jnp

def _softmax(x, axis=-1):
    return jax.nn.softmax(x, axis=axis)
def _gelu(x):
    return jax.nn.gelu(x, approximate=True)
def _silu(x):
    return jax.nn.silu(x)
def _sigmoid(x):
    return jax.nn.sigmoid(x)
def _layernorm(x, axis=-1, eps=1e-5):
    m = jnp.mean(x, axis=axis, keepdims=True)
    v = jnp.var(x, axis=axis, keepdims=True)
    return (x - m) / jnp.sqrt(v + eps)
def _scatter_add(tgt, idx, src, axis=0):
    return tgt.at[idx].add(src)
def _segment_sum(src, seg, n):
    return jax.ops.segment_sum(src, seg, n)

kernel_name = 'mk_conv_preact_d2_conv_nchw192_8196a7'

def setup_inputs(seed: int = 0):
    np.random.seed(seed)
    _w = jnp.asarray
    def _rec_inputs():
        import jax
        import jax.numpy as jnp
        _gk = jax.random.key(seed)
        x = -0.0001836 + 1 * jax.random.normal(jax.random.fold_in(_gk, 1), (4, 192, 256, 256), jnp.float32)
        return x
    x = _rec_inputs()
    def _L0_conv_setup():
        import jax, jax.numpy as jnp
        import numpy as np
        P = 8
        DIM = 192
        key = jax.random.key(seed)
        k1, k2 = jax.random.split(key)
        x = jax.random.normal(k1, (8, DIM, 256, 256), dtype=jnp.float32)
        w_proj = jax.random.normal(k2, (DIM, DIM), dtype=jnp.float32) * 0.05
        fft_filter = jnp.ones((DIM, 1, 1, P, P // 2 + 1), dtype=jnp.float32)
        return {'x': x, 'w_proj': w_proj, 'fft_filter': fft_filter}
    _L0_conv_all = _L0_conv_setup()
    _L0_conv_in = {k: v for k, v in _L0_conv_all.items() if k in ('w_proj', 'fft_filter', )}
    del _L0_conv_all

    def _L1_conv_setup():
        import jax, jax.numpy as jnp
        import numpy as np
        P = 8
        DIM = 192
        key = jax.random.key(seed)
        k1, k2 = jax.random.split(key)
        x = jax.random.normal(k1, (8, DIM, 256, 256), dtype=jnp.float32)
        w_proj = jax.random.normal(k2, (DIM, DIM), dtype=jnp.float32) * 0.05
        fft_filter = jnp.ones((DIM, 1, 1, P, P // 2 + 1), dtype=jnp.float32)
        return {'x': x, 'w_proj': w_proj, 'fft_filter': fft_filter}
    _L1_conv_all = _L1_conv_setup()
    _L1_conv_in = {k: v for k, v in _L1_conv_all.items() if k in ('w_proj', 'fft_filter', )}
    del _L1_conv_all

    return {
        "x": x,
        "L0_conv_w_proj": _L0_conv_in["w_proj"],
        "L0_conv_fft_filter": _L0_conv_in["fft_filter"],
        "L1_conv_w_proj": _L1_conv_in["w_proj"],
        "L1_conv_fft_filter": _L1_conv_in["fft_filter"],
    }

def reference(x, L0_conv_w_proj, L0_conv_fft_filter, L1_conv_w_proj, L1_conv_fft_filter):
    import jax
    import jax.numpy as jnp
    def _L0_conv_ref(x, w_proj, fft_filter):
        import jax, jax.numpy as jnp
        import numpy as np
        P = 8
        DIM = 192
        y = jnp.einsum('oc,bchw->bohw', w_proj, x)
        b, c, h, w = y.shape
        h_n = (P - h % P) % P
        w_n = (P - w % P) % P
        y = jnp.pad(y, ((0, 0), (0, 0), (0, h_n), (0, w_n)), mode='reflect')
        H, W = (y.shape[2], y.shape[3])
        yp = y.reshape(b, c, H // P, P, W // P, P).transpose(0, 1, 2, 4, 3, 5)
        f = jnp.fft.rfft2(yp.astype(jnp.float32))
        f = f * fft_filter
        yp = jnp.fft.irfft2(f, s=(P, P))
        y = yp.transpose(0, 1, 2, 4, 3, 5).reshape(b, c, H, W)
        return y[:, :, :h, :w]

    def _L1_conv_ref(x, w_proj, fft_filter):
        import jax, jax.numpy as jnp
        import numpy as np
        P = 8
        DIM = 192
        y = jnp.einsum('oc,bchw->bohw', w_proj, x)
        b, c, h, w = y.shape
        h_n = (P - h % P) % P
        w_n = (P - w % P) % P
        y = jnp.pad(y, ((0, 0), (0, 0), (0, h_n), (0, w_n)), mode='reflect')
        H, W = (y.shape[2], y.shape[3])
        yp = y.reshape(b, c, H // P, P, W // P, P).transpose(0, 1, 2, 4, 3, 5)
        f = jnp.fft.rfft2(yp.astype(jnp.float32))
        f = f * fft_filter
        yp = jnp.fft.irfft2(f, s=(P, P))
        y = yp.transpose(0, 1, 2, 4, 3, 5).reshape(b, c, H, W)
        return y[:, :, :h, :w]

    def _gn(v, G=32, eps=1e-5):
        B_, C_, H_, W_ = v.shape
        g = v.reshape(B_, G, C_ // G, H_, W_)
        m = jnp.mean(g, axis=(2, 3, 4), keepdims=True)
        s = jnp.var(g, axis=(2, 3, 4), keepdims=True)
        return ((g - m) / jnp.sqrt(s + eps)).reshape(v.shape)

    def _ln_c(v, eps=1e-6):
        m = jnp.mean(v, axis=1, keepdims=True)
        s = jnp.var(v, axis=1, keepdims=True)
        return (v - m) / jnp.sqrt(s + eps)

    def _ln_t(v, eps=1e-5):
        m = jnp.mean(v, axis=-1, keepdims=True)
        s = jnp.var(v, axis=-1, keepdims=True)
        return (v - m) / jnp.sqrt(s + eps)

    def _to_tokens(v):
        B_, C_, H_, W_ = v.shape
        return v.reshape(B_, C_, H_ * W_).transpose(0, 2, 1)
    def _from_tokens(t, like):
        B_, C_, H_, W_ = like.shape
        return t.transpose(0, 2, 1).reshape(B_, C_, H_, W_)

    x = x + _L0_conv_ref(_gn(x), L0_conv_w_proj, L0_conv_fft_filter)
    x = x + _L1_conv_ref(_gn(x), L1_conv_w_proj, L1_conv_fft_filter)
    return x


_drawn_inputs = setup_inputs


def setup_inputs(seed=0):
    import zlib

    import numpy as np

    out = dict(_drawn_inputs(seed))
    spreads = {'L0_conv_fft_filter': (1.0, 0.2), 'L1_conv_fft_filter': (1.0, 0.2)}
    factors = {}
    for name, (base, spread) in spreads.items():
        noise = np.random.default_rng([zlib.crc32(name.encode()), seed]).standard_normal(out[name].shape)
        drawn = base * np.exp(spread * noise) if base else spread * noise
        out[name] = jnp.asarray(drawn.astype(out[name].dtype))
    for name, factor in factors.items():
        out[name] = (out[name] * factor).astype(out[name].dtype)
    return out
```

```python
from contextlib import ExitStack

import concourse.bass as bass
from concourse import mybir

F32 = mybir.dt.float32
F16 = mybir.dt.float16
ALU = mybir.AluOpType
ACT = mybir.ActivationFunctionType
AX = mybir.AxisListType

BATCH, CH, HEIGHT, WIDTH = 4, 192, 256, 256
P = 128
CA, CB = 128, CH - 128
PATCH = 8
SLOTS = PATCH * PATCH
TILE = 128
HALF = TILE // 2
TPB = (HEIGHT // PATCH) * (WIDTH // PATCH) // TILE
TILES = BATCH * TPB
PARTS = 8
SPP = SLOTS // PARTS
UNIT = SPP // 2
SINGLES, PAIRS = 4, 30
FREQS = SINGLES + PAIRS
GROUPS = 32
CPG = CH // GROUPS
POS = HEIGHT * WIDTH
STAT_CHUNK = 1536
BN = 512
XCOLS = CH * POS // P
CHUNKS = XCOLS // STAT_CHUNK
BNPC = STAT_CHUNK // BN
EPS = 1e-5
XSCALE = 8.0
WSCALE = 256.0
TINY = 1e-30
NEWPAIRS = 8
CONSTS = 15
PREP_STEPS = 30
LINKS0, LINKS1 = 13, 26
COUPLES = TILE // 4
TRING = 16

MIX_AHEAD = 4
EVAC_AHEAD = 2
STAT_AHEAD = 2
SQ_AHEAD = 1
INV_AHEAD = TRING
TBANK_AHEAD = 2
OBANK_AHEAD = 2


def build(nc, x_stat, x_patch, w0, w1, wt0, wt1, f0, f1, fwd, inv, ident, gmats, smats, out):
    x1a = nc.dram_tensor("x1a_scratch", (TILES, PARTS, P, SPP * TILE), F32, kind="Internal").ap()
    x1b = nc.dram_tensor("x1b_scratch", (TILES, PARTS, P, SPP * HALF), F32, kind="Internal").ap()
    gn_dram = nc.dram_tensor("gn_scratch", (2, CH, FREQS), F32, kind="Internal").ap()

    ctx = ExitStack()
    with ctx:
        def sb(name, shape, dt=F32):
            return ctx.enter_context(nc.sbuf_tensor(name, shape, dt))

        def sem(name):
            return ctx.enter_context(nc.semaphore(name))

        XA = [sb(f"XA{i}", [P, SLOTS, TILE]) for i in range(2)]
        XB = [sb(f"XB{i}", [P, SLOTS, HALF]) for i in range(2)]
        WA = sb("WA", [P, FREQS, 2, CH], F16)
        WB = sb("WB", [P, FREQS, 2, CH], F16)
        highA = sb("highA", [P, 2, SPP, TILE], F16)
        lowA = sb("lowA", [P, 2, SPP, TILE], F16)
        splitB = sb("splitB", [P, 2, SPP, TILE], F16)
        NX = 4
        XIN = NEWPAIRS * CH
        arena = sb("arena", [P, NX * XIN + 2 * STAT_CHUNK + CHUNKS * BNPC * 6])
        xin = arena[:, 0:NX * XIN].rearrange("p (s q c) -> p s q c", s=NX, q=NEWPAIRS)
        statin = arena[:, NX * XIN:NX * XIN + 2 * STAT_CHUNK].rearrange("p (s n) -> p s n", s=2)
        bn = arena[:, NX * XIN + 2 * STAT_CHUNK:]
        COUPLE = 2 * CH
        tring = arena[:, 0:TRING * COUPLE].rearrange("p (s n) -> p s n", s=TRING)
        oring = arena[:, TRING * COUPLE:(TRING + 8) * COUPLE].rearrange("p (s j n) -> p s j n", s=2, j=4)

        fwd_sb = sb("fwd_sb", [P, P])
        inv_sb = sb("inv_sb", [P, P])
        ident_sb = fwd_sb
        gm = sb("gm", [P, 4, P])
        sm = gm[:, 0:3, :]
        centA = sb("centA", [P, TILE])
        centB = sb("centB", [P, HALF])
        sqA = sb("sqA", [P, TILES * PARTS])
        sqB = sb("sqB", [P, TILES * PARTS])
        dcA = sb("dcA", [P, TILES * 6])
        dcB = sb("dcB", [P, TILES * 6])
        scale = sb("scale", [P, 2, 2])
        rcur = sb("rcur", [P, 2])
        mcur = sb("mcur", [P, 2])
        r1 = sb("r1", [P, 2, BATCH])
        m1 = sb("m1", [P, 2, BATCH])
        work = sb("work", [P, 12, 2 * BATCH])

        psMA = ctx.enter_context(nc.psum_tensor("psMA", [P, 2, 512], F32))
        psMB = ctx.enter_context(nc.psum_tensor("psMB", [P, 2, 512], F32))
        psC = ctx.enter_context(nc.psum_tensor("psC", [P, 3, 512], F32))
        psS = ctx.enter_context(nc.psum_tensor("psS", [P, 512], F32))
        psFA, psFB = psC[:, 0:2, :], psC[:, 2, :]
        psT = psC[:, 0:2, :]
        psO = [psC[:, 2, 0:COUPLE], psS[:, 0:COUPLE]]

        wnat = XA[0][:, 0:8, :].rearrange("p a b -> p (a b)")[:, 0:4 * CH].rearrange("p (l c) -> p l c", l=4)
        filt = XA[0][:, 8:10, :].rearrange("p a b -> p (a b)")[:, 0:160].rearrange("p (l h w) -> p l h w", l=4, h=PATCH)
        geff = XA[0][:, 10:12, :].rearrange("p a b -> p (a b)")[:, 0:4 * FREQS].rearrange("p (l k) -> p l k", l=4)
        gnorm = XA[0][:, 12:14, :].rearrange("p a b -> p (a b)")[:, 0:4 * FREQS].rearrange("p (l k) -> p l k", l=4)
        KH = FREQS // 2
        gall = XA[1][:, :, :].rearrange("p a b -> p (a b)")[:, 0:CH * FREQS].rearrange("p (o k) -> p k o", k=FREQS)
        wprod = XB[1][:, :, :].rearrange("p a b -> p (a b)")[:, 0:KH * CH].rearrange("p (k o) -> p k o", k=KH)
        wtr = XB[1][:, :, :].rearrange("p a b -> p (a b)")[:, KH * CH:KH * CH + 2 * CH].rearrange("p (r o) -> p r o", r=2)

        const_in = sem("const_in")
        prep = sem("prep")
        gn_out = sem("gn_out")
        w_in = sem("w_in")
        w_prod = sem("w_prod")
        w_high = sem("w_high")
        w_low = sem("w_low")
        xin_in = [sem(f"xin_in{i}") for i in range(NX)]
        stat_in = [sem(f"stat_in{i}") for i in range(2)]
        stat_used = sem("stat_used")
        step = sem("step")
        s_dve = sem("s_dve")
        s_pe = sem("s_pe")
        s_act = sem("s_act")
        image_begun = sem("image_begun")
        norm_ready = sem("norm_ready")
        fwd_ready = sem("fwd_ready")
        fwd_taken = sem("fwd_taken")
        cent = sem("cent")
        high_ready = sem("high_ready")
        low_ready = sem("low_ready")
        mix_ready = sem("mix_ready")
        mix_taken = sem("mix_taken")
        x_out = [sem(f"x_out{i}") for i in range(2)]
        x_free = sem("x_free")
        sq_done = sem("sq_done")
        x_in = [[sem(f"x_in{i}_{u}") for u in range(PARTS)] for i in range(2)]
        t_ready = sem("t_ready")
        t_taken = sem("t_taken")
        inv_ready = sem("inv_ready")
        o_taken = sem("o_taken")
        o_out = [sem(f"o_out{i}") for i in range(2)]
        o_free = sem("o_free")

        def part(t, u):
            return t[:, SPP * u:SPP * (u + 1), :]

        def act_high(act, n, u, layer):
            par, slot = n[1], u % 2
            a, b = part(XA[par], u), part(XB[par], u)
            base = layer * TILES
            act.wait_ge(mix_ready, n[0] * 16 + base * 16 + 2 * u - 2 + MIX_AHEAD)
            if layer == 0:
                act.wait_ge(sq_done, n[0] * 8 + max(u - 1, 0) + SQ_AHEAD)
            else:
                act.wait_ge(x_in[par][u], n[2] * 32 + 32)
            first = 0
            if u == 0:
                first = 1
                act.activation(centA[:], a[:, 0, :], ACT.Identity, bias=mcur[:, 0:1])
                act.activation(centB[:], b[:, 0, :], ACT.Identity, bias=mcur[:, 1:2]).then_inc(cent, 1)
                act.wait_ge(cent, n[0] + base + 1)
                act.activation(highA[:, slot, 0, :], centA[:], ACT.Copy, scale=rcur[:, 0:1])
                act.activation(splitB[0:64, slot, 0, 0:HALF], centB[0:64, :], ACT.Copy, scale=rcur[0:64, 1:2])
                act.activation(splitB[64:P, slot, 0, HALF:TILE], centB[64:P, :], ACT.Copy, scale=rcur[64:P, 1:2])
            act.activation(highA[:, slot, first:, :], a[:, first:, :], ACT.Copy, scale=rcur[:, 0:1])
            act.activation(splitB[0:64, slot, first:, 0:HALF], b[0:64, first:, :], ACT.Copy, scale=rcur[0:64, 1:2])
            act.activation(splitB[64:P, slot, first:, HALF:TILE], b[64:P, first:, :], ACT.Copy,
                           scale=rcur[64:P, 1:2]).then_inc(high_ready, 1)

        def dve_low(dve, n, u, base):
            par, slot = n[1], u % 2
            a, b = part(XA[par], u), part(XB[par], u)
            dve.wait_ge(high_ready, n[0] * 8 + base * 8 + u + 1)

            def low(o, v, r, h):
                return dve.scalar_tensor_tensor(out=o, in0=v, scalar=r, in1=h, op0=ALU.mult, op1=ALU.subtract)
            first = 0
            if u == 0:
                first = 1
                low(lowA[:, slot, 0, :], centA[:], rcur[:, 0:1], highA[:, slot, 0, :])
                low(splitB[64:P, slot, 0, 0:HALF], centB[0:64, :], rcur[0:64, 1:2], splitB[0:64, slot, 0, 0:HALF])
                low(splitB[0:64, slot, 0, HALF:TILE], centB[64:P, :], rcur[64:P, 1:2], splitB[64:P, slot, 0, HALF:TILE])
            low(lowA[:, slot, first:, :], a[:, first:, :], rcur[:, 0:1], highA[:, slot, first:, :])
            low(splitB[64:P, slot, first:, 0:HALF], b[0:64, first:, :], rcur[0:64, 1:2],
                splitB[0:64, slot, first:, 0:HALF])
            low(splitB[0:64, slot, first:, HALF:TILE], b[64:P, first:, :], rcur[64:P, 1:2],
                splitB[64:P, slot, first:, HALF:TILE]).then_inc(low_ready, 1)

        def dve_update(dve, n, u, h, layer, base):
            par, v = n[1], 2 * u + h
            dve.wait_ge(mix_ready, n[0] * 16 + base * 16 + v + 1 + MIX_AHEAD)
            xa = XA[par][:, UNIT * v:UNIT * (v + 1), :].rearrange("p a b -> p (a b)")
            xb = XB[par][:, UNIT * v:UNIT * (v + 1), :].rearrange("p a b -> p (a b)")
            dve.scalar_tensor_tensor(out=xa, in0=psMA[:, h, :], scalar=scale[:, layer, 0:1], in1=xa,
                                     op0=ALU.mult, op1=ALU.add)
            dve.scalar_tensor_tensor(out=xb, in0=psMB[:, h, 0:UNIT * HALF], scalar=scale[:, layer, 1:2], in1=xb,
                                     op0=ALU.mult, op1=ALU.add).then_inc(mix_taken, 1)

        def pe_mix(pe, n, u, base):
            slot = u % 2
            pe.wait_ge(low_ready, n[0] * 8 + base * 8 + u + 1)
            for h in range(2):
                v = 2 * u + h
                pe.wait_ge(mix_taken, n[0] * 16 + base * 16 + v - 1 + EVAC_AHEAD)
                if v == 0:
                    blocks = [(s, s, 1) for s in range(SINGLES)]
                else:
                    first = SINGLES + 2 * (v - 1)
                    blocks = [(first, 0, 2), (first + 1, 2, 2)]
                for w, s, m in blocks:
                    src = slice(UNIT * h + s, UNIT * h + s + m)
                    ins = [(WA[:, w, 0, :], highA), (WA[:, w, 1, :], highA), (WA[:, w, 0, :], lowA),
                           (WB[:, w, 0, :], splitB), (WB[:, w, 1, :], splitB)]
                    for i, (wt, xs) in enumerate(ins):
                        pe.matmul(psMA[:, h, s * TILE:(s + m) * TILE], wt[:, 0:CA], xs[:, slot, src, :],
                                  start=(i == 0), stop=(i == len(ins) - 1))
                for w, s, m in blocks:
                    src = slice(UNIT * h + s, UNIT * h + s + m)
                    ins = [(WA[:, w, 0, :], highA), (WA[:, w, 1, :], highA), (WA[:, w, 0, :], lowA),
                           (WB[:, w, 0, :], splitB), (WB[:, w, 1, :], splitB)]
                    for i, (wt, xs) in enumerate(ins):
                        for q in range(2):
                            mm = pe.matmul(psMB[64 * q:64 * q + 64, h, s * HALF:(s + m) * HALF], wt[:, CA:CH],
                                           xs[:, slot, src, HALF * q:HALF * q + HALF],
                                           start=(i == 0), stop=(i == len(ins) - 1))
                mm.then_inc(mix_ready, 1)

        class Count:
            def __init__(self):
                self.n = 0

            def next(self, k=1):
                self.n += k
                return self.n

        def dve_rstd(dve, link, var, n, out_r, act_value):
            ve, root, r, t = (work[:, i, 0:n] for i in (4, 5, 6, 7))
            link(dve.tensor_scalar(ve, var, EPS, None, ALU.add))
            dve.sem_inc(s_dve, 1)
            dve.wait_ge(s_act, act_value)
            link(dve.reciprocal(r, root))
            link(dve.tensor_tensor(t, r, r, ALU.mult))
            link(dve.tensor_tensor(t, t, ve, ALU.mult))
            link(dve.tensor_scalar(t, t, -0.5, 1.5, ALU.mult, ALU.add))
            link(dve.tensor_tensor(t, t, r, ALU.mult))
            link(dve.tensor_scalar(out_r, t, XSCALE, None, ALU.mult))

        def load_weights(sp, layer):
            wt = (wt0, wt1)[layer]
            sp.dma_start(gall.rearrange("p k o -> p o k"),
                         gn_dram[layer:layer + 1].rearrange("a o k -> a (o k)").to_broadcast([P, CH * FREQS])
                         .rearrange("p (o k) -> p o k", k=FREQS)).then_inc(w_in, 16)
            sp.dma_start(wtr[:, 0, :], wt[0:CA, :]).then_inc(w_in, 16)
            sp.dma_start(wtr[0:CB, 1, :], wt[CA:CH, :]).then_inc(w_in, 16)
            sp.dma_start(wtr[CB:P, 1, :], wt[CA:CH, :]).then_inc(w_in, 16)

        def dve_weights(dve, layer):
            dve.wait_ge(w_in, 64 * (layer + 1))
            for i in range(4):
                rows, ks = i // 2, slice(KH * (i % 2), KH * (i % 2) + KH)
                W = (WA, WB)[rows]
                w = wtr[:, rows, :].rearrange("p (a o) -> p a o", a=1).to_broadcast([P, KH, CH])
                dve.tensor_tensor(wprod, gall[:, ks, :], w, ALU.mult).then_inc(w_prod, 1)
                dve.wait_ge(w_prod, 4 * layer + i + 1)
                dve.wait_ge(w_high, 4 * layer + i + 1)
                dve.tensor_tensor(W[:, ks, 1, :], wprod, W[:, ks, 0, :], ALU.subtract).then_inc(w_low, 1)
                dve.wait_ge(w_low, 4 * layer + i + 1)

        def act_weights(act, layer):
            for i in range(4):
                ks = slice(KH * (i % 2), KH * (i % 2) + KH)
                act.wait_ge(w_prod, 4 * layer + i + 1)
                act.copy((WA, WB)[i // 2][:, ks, 0, :], wprod).then_inc(w_high, 1)

        with nc.Block() as block:
            def pairs(eng, emit):
                with eng.Fori(0, BATCH - 1) as b:
                    emit("begin", b, None)
                    with eng.Fori(0, TPB // 2) as t:
                        emit("stat", b, t)
                emit("begin", BATCH - 1, None)
                with eng.Fori(0, TPB // 2 - 1) as t:
                    emit("plain", BATCH - 1, t)
                emit("last", BATCH - 1, TPB // 2 - 1)

            def tile(b, t, par):
                return (b * TPB + t * 2 + par, par, b * (TPB // 2) + t)

            @block.sync
            def _(sp):
                for i, w in enumerate((w0, w1)):
                    sp.dma_start(wnat[:, 2 * i, :], w[0:CA, :]).then_inc(const_in, 16)
                    sp.dma_start(wnat[0:CB, 2 * i + 1, :], w[CA:CH, :]).then_inc(const_in, 16)
                    sp.dma_start(wnat[CB:P, 2 * i + 1, :], w[CA:CH, :]).then_inc(const_in, 16)
                for i, f in enumerate((f0, f1)):
                    fv = f.rearrange("o (h w) -> o h w", h=PATCH)
                    sp.dma_start(filt[:, 2 * i, :, :], fv[0:CA]).then_inc(const_in, 16)
                    sp.dma_start(filt[0:CB, 2 * i + 1, :, :], fv[CA:CH]).then_inc(const_in, 16)
                    sp.dma_start(filt[CB:P, 2 * i + 1, :, :], fv[CA:CH]).then_inc(const_in, 16)
                sp.dma_start(fwd_sb[:], fwd).then_inc(const_in, 16)
                sp.dma_start(inv_sb[:], inv).then_inc(const_in, 16)
                sp.dma_start(sm, smats).then_inc(const_in, 16)
                for g in range(NX):
                    sp.dma_start(xin[:, g], x_patch[0, g]).then_inc(xin_in[g], 16)
                sp.wait_ge(prep, PREP_STEPS)
                for i in range(2):
                    sp.dma_start(gn_dram[i, 0:CA, :], gnorm[:, 2 * i, :]).then_inc(gn_out, 16)
                    sp.dma_start(gn_dram[i, CA:CH, :], gnorm[0:CB, 2 * i + 1, :]).then_inc(gn_out, 16)
                sp.wait_ge(gn_out, 64)
                load_weights(sp, 0)
                with sp.Fori(0, CHUNKS // 2) as c:
                    for s in range(2):
                        sp.wait_ge(stat_used, c * 2 + s - 1 + STAT_AHEAD)
                        sp.dma_start(statin[:, s, :], x_stat[0, :, bass.ds((c * 2 + s) * STAT_CHUNK, STAT_CHUNK)]
                                     ).then_inc(stat_in[s], 16)
                for g in range(NX, PARTS + NX):
                    sp.wait_ge(fwd_ready, 3 * (g - NX) + 3)
                    sp.dma_start(xin[:, g % NX], x_patch[g // PARTS, g % PARTS]).then_inc(xin_in[g % NX], 16)

                def emit(kind, b, t):
                    if kind == "begin":
                        return
                    for par in range(2):
                        n = tile(b, t, par)
                        for u in range(PARTS):
                            ahead = u + NX
                            if kind != "last" or (par == 0 and ahead < PARTS):
                                sp.wait_ge(fwd_ready, n[0] * 24 + 24 + 3 * u + 3)
                                sp.dma_start(xin[:, u % NX],
                                             x_patch[bass.ds(n[0] + 1 + ahead // PARTS, 1), ahead % PARTS]
                                             .rearrange("a p q c -> (a p) q c")).then_inc(xin_in[u % NX], 16)
                            if kind == "stat":
                                s = u % 2
                                chunk = b * CHUNKS + t * 16 + par * 8 + u
                                sp.wait_ge(stat_used, chunk + CHUNKS - 1 + STAT_AHEAD)
                                sp.dma_start(statin[:, s, :],
                                             x_stat[bass.ds(b + 1, 1), :, bass.ds((t * 16 + par * 8 + u) * STAT_CHUNK, STAT_CHUNK)]
                                             .rearrange("a p n -> (a p) n")).then_inc(stat_in[s], 16)
                            sp.wait_ge(mix_taken, n[0] * 16 + 2 * u + 2 + EVAC_AHEAD)
                            sp.dma_start(x1a[bass.ds(n[0], 1), u].rearrange("a p n -> (a p) n"),
                                         part(XA[par], u).rearrange("p a b -> p (a b)")).then_inc(x_out[par], 16)
                            sp.dma_start(x1b[bass.ds(n[0], 1), u].rearrange("a p n -> (a p) n"),
                                         part(XB[par], u).rearrange("p a b -> p (a b)")).then_inc(x_out[par], 16)
                pairs(sp, emit)
                for par in range(2):
                    sp.wait_ge(x_out[par], TILES // 2 * PARTS * 32)

            @block.gpsimd
            def _(pool):
                pool.sem_inc(x_free, 1)
                with pool.Fori(0, TILES // 2) as i:
                    for par in range(2):
                        pool.wait_ge(x_out[par], i * (PARTS * 32) + PARTS * 32)
                        pool.sem_inc(x_free, 1)

            @block.scalar
            def _(act):
                act.sem_inc(sq_done, SQ_AHEAD)
                act_weights(act, 0)

                def take_fwd(par, u, base):
                    for h in range(2):
                        act.wait_ge(fwd_ready, base + 3 * u + 1 + h)
                        act.copy(XA[par][:, :, HALF * h + 8 * u:HALF * h + 8 * u + 8]
                                 .rearrange("p k (q a) -> p k q a", a=2),
                                 psFA[:, h, :].rearrange("p (q k a) -> p k q a", q=4, a=2)).then_inc(fwd_taken, 1)
                    act.wait_ge(fwd_ready, base + 3 * u + 3)
                    act.copy(XB[par][:, :, 8 * u:8 * u + 8].rearrange("p k (q a) -> p k q a", a=2),
                             psFB.rearrange("p (q k a) -> p k q a", q=4, a=2)).then_inc(fwd_taken, 1)

                act.wait_ge(w_low, 4)
                for u in range(PARTS):
                    take_fwd(0, u, 0)

                def squares(n, u):
                    par = n[1]
                    act.wait_ge(mix_taken, n[0] * 16 + 2 * u + 2 + EVAC_AHEAD)
                    first = 1 if u == 0 else 0
                    act.activation(highA[:, u % 2, first:, :], part(XA[par], u)[:, first:, :], ACT.Square,
                                   accum_out=sqA[:, bass.ds(n[0] * 8 + u, 1)])
                    act.activation(splitB[:, u % 2, first:, 0:HALF], part(XB[par], u)[:, first:, :], ACT.Square,
                                   accum_out=sqB[:, bass.ds(n[0] * 8 + u, 1)]).then_inc(sq_done, 1)

                def emit(kind, b, t):
                    if kind == "begin":
                        act.wait_ge(s_dve, b * 3 + 3)
                        act.activation(work[:, 5, 0:2], work[:, 4, 0:2], ACT.Sqrt).then_inc(s_act, 1)
                        act.wait_ge(norm_ready, b + 1)
                        return
                    for par in range(2):
                        n = tile(b, t, par)
                        act.wait_ge(fwd_taken, n[0] * 24 + 24)
                        act_high(act, n, 0, 0)
                        for u in range(PARTS):
                            if kind != "last" or par == 0:
                                if u == 0:
                                    act.wait_ge(x_free, n[0] + 1)
                                take_fwd(1 - par, u, n[0] * 24 + 24)
                            if u >= 1:
                                squares(n, u - 1)
                            if u + 1 < PARTS:
                                act_high(act, n, u + 1, 0)
                        squares(n, PARTS - 1)
                pairs(act, emit)

            @block.tensor
            def _(pe):
                pe.sem_inc(mix_ready, MIX_AHEAD)
                pe.wait_ge(const_in, 16 * CONSTS)

                def forward(u, base, loads, first=False):
                    pe.wait_ge(xin_in[u % NX], loads + 16 * (u // NX) + 16)
                    src = xin[:, u % NX]
                    for h in range(2):
                        if not (first and u == 0):
                            pe.wait_ge(fwd_taken, base + 3 * (u - 1) + 1 + h)
                        for q in range(4):
                            mm = pe.matmul(psFA[:, h, q * P:(q + 1) * P], src[:, 4 * h + q, 0:CA], fwd_sb[:],
                                           start=True, stop=True)
                        mm.then_inc(fwd_ready, 1)
                    if not (first and u == 0):
                        pe.wait_ge(fwd_taken, base + 3 * u)
                    for q in range(4):
                        for h in range(2):
                            mm = pe.matmul(psFB[64 * h:64 * h + 64, q * P:(q + 1) * P], src[:, 4 * h + q, CA:CH],
                                           fwd_sb[:], start=True, stop=True)
                    mm.then_inc(fwd_ready, 1)

                for u in range(PARTS):
                    forward(u, 0, 0, first=True)

                def emit(kind, b, t):
                    if kind == "begin":
                        pe.wait_ge(s_dve, b * 3 + 1)
                        pe.matmul(psS[:, 0:1], sm[:, 0, :], work[:, 0, 0:1], start=True, stop=True).then_inc(s_pe, 1)
                        pe.wait_ge(s_dve, b * 3 + 2)
                        pe.matmul(psS[:, 0:2], sm[:, 1, :], work[:, 2, 0:2], start=True, stop=True)
                        pe.matmul(psS[:, 2:4], sm[:, 2, :], work[:, 2, 0:2], start=True, stop=True).then_inc(s_pe, 1)
                        return
                    for par in range(2):
                        n = tile(b, t, par)
                        for u in range(PARTS):
                            if kind != "last" or par == 0:
                                forward(u, n[0] * 24 + 24, n[0] * 32 + 32)
                            pe_mix(pe, n, u, 0)
                pairs(pe, emit)

            @block.vector
            def _(dve):
                dve.sem_inc(mix_taken, EVAC_AHEAD)
                dve.sem_inc(stat_used, STAT_AHEAD)
                dve.wait_ge(const_in, 16 * CONSTS)
                cnt = Count()

                def pl(ins):
                    ins.then_inc(prep, 1)
                    dve.wait_ge(prep, cnt.next())
                flat = filt.rearrange("p l h w -> p l (h w)")
                pl(dve.tensor_copy(geff[:, :, 0:2], flat[:, :, 0:21:20]))
                pl(dve.tensor_copy(geff[:, :, 2:4], flat[:, :, 4:25:20]))
                for i in range(4):
                    pl(dve.tensor_copy(geff[:, i, 4:28].rearrange("p (h w) -> p h w", w=3), filt[:, i, :, 1:4]))
                for j, kw in enumerate((0, 4)):
                    for kh in (1, 2, 3):
                        pl(dve.tensor_tensor(geff[:, :, 27 + 3 * j + kh], filt[:, :, kh, kw], filt[:, :, 8 - kh, kw],
                                             ALU.add))
                pl(dve.tensor_scalar(geff[:, :, 28:34], geff[:, :, 28:34], 0.5, None, ALU.mult))
                pl(dve.tensor_reduce(work[:, 0, 0:4], wnat, AX.X, ALU.max))
                pl(dve.tensor_reduce(work[:, 1, 0:4], wnat, AX.X, ALU.min))
                pl(dve.tensor_reduce(work[:, 2, 0:4], geff, AX.X, ALU.max))
                pl(dve.tensor_reduce(work[:, 3, 0:4], geff, AX.X, ALU.min))
                pl(dve.tensor_scalar(work[:, 1, 0:4], work[:, 1, 0:4], -1.0, None, ALU.mult))
                pl(dve.tensor_scalar(work[:, 3, 0:4], work[:, 3, 0:4], -1.0, None, ALU.mult))
                pl(dve.tensor_tensor(work[:, 0, 0:4], work[:, 0, 0:4], work[:, 1, 0:4], ALU.max))
                pl(dve.tensor_tensor(work[:, 2, 0:4], work[:, 2, 0:4], work[:, 3, 0:4], ALU.max))
                pl(dve.tensor_tensor(work[:, 0, 0:4], work[:, 0, 0:4], work[:, 2, 0:4], ALU.mult))
                pl(dve.tensor_scalar(work[:, 0, 0:4], work[:, 0, 0:4], TINY, None, ALU.max))
                pl(dve.tensor_scalar(scale[:].rearrange("p l r -> p (l r)"), work[:, 0, 0:4], 1.0 / (XSCALE * WSCALE),
                                     None, ALU.mult))
                pl(dve.reciprocal(work[:, 1, 0:4], work[:, 0, 0:4]))
                pl(dve.tensor_scalar(work[:, 1, 0:4], work[:, 1, 0:4], WSCALE, None, ALU.mult))
                for i in range(4):
                    pl(dve.tensor_scalar(gnorm[:, i, :], geff[:, i, :], work[:, 1, i:i + 1], None, ALU.mult))
                assert cnt.n == PREP_STEPS
                dve_weights(dve, 0)

                def stats(s, value, index):
                    dve.wait_ge(stat_in[s], value)
                    for j in range(BNPC):
                        ins = dve.bn_stats(bn[:, bass.ds(index * (BNPC * 6) + 6 * j, 6)],
                                           statin[:, s, BN * j:BN * (j + 1)])
                    ins.then_inc(stat_used, 1)
                with dve.Fori(0, CHUNKS // 2) as c:
                    for s in range(2):
                        stats(s, c * 16 + 16, c * 2 + s)

                def emit(kind, b, t):
                    if kind == "begin":
                        dve.wait_ge(stat_used, b * CHUNKS + CHUNKS + STAT_AHEAD)
                        dve.sem_inc(image_begun, 1)
                        k = Count()

                        def link(ins):
                            ins.then_inc(step, 1)
                            dve.wait_ge(step, b * LINKS0 + k.next())
                        link(dve.bn_aggr(work[:, 0, 0:2], bn))
                        dve.sem_inc(s_dve, 1)
                        dve.wait_ge(s_pe, b * 2 + 1)
                        d = work[:, 1, 0:1]
                        link(dve.tensor_tensor(d, work[:, 0, 0:1], psS[:, 0:1], ALU.subtract))
                        link(dve.tensor_copy(work[:, 2, 0:1], work[:, 0, 0:1]))
                        link(dve.scalar_tensor_tensor(out=work[:, 2, 1:2], in0=d, scalar=d, in1=work[:, 0, 1:2],
                                                      op0=ALU.mult, op1=ALU.add))
                        dve.sem_inc(s_dve, 1)
                        dve.wait_ge(s_pe, b * 2 + 2)
                        link(dve.tensor_copy(work[:, 3, 0:4], psS[:, 0:4]))
                        mv = work[:, 3, 0:4].rearrange("p (r m) -> p m r", m=2)
                        link(dve.tensor_scalar(mcur[:], mv[:, 0, :], -float(PATCH), None, ALU.mult))
                        dve_rstd(dve, link, mv[:, 1, :], 2, rcur[:], b + 1)
                        assert k.n == LINKS0, k.n
                        dve.sem_inc(norm_ready, 1)
                        return
                    for par in range(2):
                        n = tile(b, t, par)
                        dve_low(dve, n, 0, 0)
                        for u in range(PARTS):
                            dve_update(dve, n, u, 0, 0, 0)
                            if u == 0:
                                dve.wait_ge(mix_taken, n[0] * 16 + 1 + EVAC_AHEAD)
                                dve.bn_stats(dcA[:, bass.ds(n[0] * 6, 6)], XA[par][:, 0, :])
                                dve.bn_stats(dcB[:, bass.ds(n[0] * 6, 6)], XB[par][:, 0, :])
                            if u + 1 < PARTS:
                                dve_low(dve, n, u + 1, 0)
                            dve_update(dve, n, u, 1, 0, 0)
                            if kind == "stat":
                                c = t * 16 + par * 8 + u
                                stats(u % 2, (b * CHUNKS + t * 16 + CHUNKS) * 8 + (par * 4 + u // 2) * 16 + 16, c)
                pairs(dve, emit)

        with nc.Block() as block:
            def images(eng, emit):
                emit("begin", 0, None)
                emit("first", 0, 0)
                with eng.Fori(1, TPB // 2) as t:
                    emit("pair", 0, t)
                with eng.Fori(1, BATCH - 1) as b:
                    emit("begin", b, None)
                    with eng.Fori(0, TPB // 2) as t:
                        emit("pair", b, t)
                emit("begin", BATCH - 1, None)
                with eng.Fori(0, TPB // 2 - 1) as t:
                    emit("pair", BATCH - 1, t)
                emit("last", BATCH - 1, TPB // 2 - 1)

            def order(u):
                if u == 0:
                    return [("T", c) for c in range(8)] + [("I", c) for c in range(4)]
                if u < 4:
                    return [x for i in range(4) for x in (("I", 4 * u + i), ("T", 8 * u + 2 * i), ("T", 8 * u + 2 * i + 1))]
                return [("I", 4 * u + i) for i in range(4)]

            @block.sync
            def _(sp):
                sp.dma_start(ident_sb[:], ident).then_inc(const_in, 16)
                sp.dma_start(gm[:], gmats).then_inc(const_in, 16)
                load_weights(sp, 1)

                def load(n, u, par):
                    sp.dma_start(part(XA[par], u).rearrange("p a b -> p (a b)"),
                                 x1a[bass.ds(n, 1), u].rearrange("a p n -> (a p) n")).then_inc(x_in[par][u], 16)
                    sp.dma_start(part(XB[par], u).rearrange("p a b -> p (a b)"),
                                 x1b[bass.ds(n, 1), u].rearrange("a p n -> (a p) n")).then_inc(x_in[par][u], 16)
                for u in range(PARTS):
                    load(0, u, 0)
                sp.wait_ge(w_low, 8)

                def store(n, u):
                    sp.wait_ge(o_taken, (n[0] - 1) * 32 + 4 * u + 4 + OBANK_AHEAD)
                    sp.dma_start(out[bass.ds(n[0] - 1, 1), u].rearrange("a p j n -> (a p) (j n)"),
                                 oring[:, u % 2].rearrange("p j n -> p (j n)")).then_inc(o_out[u % 2], 16)

                def emit(kind, b, t):
                    if kind == "begin":
                        return
                    for par in range(2):
                        n = tile(b, t, par)
                        before = kind != "first" or par == 1
                        for u in range(PARTS):
                            if u == 3 and (kind != "last" or par == 0):
                                if before:
                                    sp.wait_ge(t_ready, n[0] * 32)
                                for w in range(PARTS):
                                    load(n[0] + 1, w, 1 - par)
                            if before:
                                store(n, u)
                images(sp, emit)
                for u in range(PARTS):
                    store((TILES, 0, TILES // 2), u)
                for s in range(2):
                    sp.wait_ge(o_out[s], TILES * PARTS // 2 * 16)

            @block.gpsimd
            def _(pool):
                pool.sem_inc(o_free, 2)
                with pool.Fori(0, TILES * PARTS // 2) as i:
                    for s in range(2):
                        pool.wait_ge(o_out[s], i * 16 + 16)
                        pool.sem_inc(o_free, 1)

            @block.scalar
            def _(act):
                act.sem_inc(t_taken, TBANK_AHEAD)
                act.sem_inc(o_taken, OBANK_AHEAD)
                act.wait_ge(s_dve, 3 * BATCH + 3)
                act.activation(work[:, 5, 0:8], work[:, 4, 0:8], ACT.Sqrt).then_inc(s_act, 1)
                act_weights(act, 1)

                def after(u, before):
                    c0 = before * COUPLES
                    for what, c in order(u):
                        if what == "T":
                            act.wait_ge(t_ready, c0 + c + 1)
                            act.wait_ge(inv_ready, c0 + c + 1 - TRING + INV_AHEAD)
                            act.copy(tring[:, c % TRING, :], psT[:, c % 2, 0:COUPLE]).then_inc(t_taken, 1)
                        else:
                            act.wait_ge(inv_ready, c0 + c + 1 + INV_AHEAD)
                            if c % 4 == 0:
                                act.wait_ge(o_free, before * PARTS + c // 4 + 1)
                            act.copy(oring[:, u % 2, c % 4, :], psO[c % 2]).then_inc(o_taken, 1)

                def emit(kind, b, t):
                    if kind == "begin":
                        act.wait_ge(norm_ready, b + BATCH + 1)
                        return
                    for par in range(2):
                        n = tile(b, t, par)
                        act_high(act, n, 0, 1)
                        for u in range(PARTS):
                            if u + 1 < PARTS:
                                act_high(act, n, u + 1, 1)
                            if kind != "first" or par == 1:
                                after(u, n[0] - 1)

                images(act, emit)
                for u in range(PARTS):
                    after(u, TILES - 1)

            @block.tensor
            def _(pe):
                pe.sem_inc(inv_ready, INV_AHEAD)
                pe.wait_ge(const_in, 16 * (CONSTS + 2))
                for i in range(2):
                    pe.wait_ge(s_dve, 3 * BATCH + 1 + i)
                    src = work[:, (0, 2)[i], 0:8]
                    for j in range(2):
                        pe.matmul(psS[:, BATCH * j:BATCH * (j + 1)], gm[:, 2 * j, :], src[:, 0:BATCH],
                                  start=True, stop=False)
                        mm = pe.matmul(psS[:, BATCH * j:BATCH * (j + 1)], gm[:, 2 * j + 1, :], src[:, BATCH:2 * BATCH],
                                       start=False, stop=True)
                    mm.then_inc(s_pe, 1)
                pe.wait_ge(s_dve, 3 * BATCH + 3)

                def after(u, n0, buf, ready):
                    for what, c in order(u):
                        if what == "T":
                            if c == 0:
                                pe.wait_ge(mix_taken, ready)
                            pe.wait_ge(t_taken, n0 * 32 + c - 1 + TBANK_AHEAD)
                            dst = psT[:, c % 2, :]
                            flatA = XA[buf][:].rearrange("p k n -> p (k n)")
                            flatB = XB[buf][:].rearrange("p k n -> p (k n)")
                            for e in range(2):
                                pe.transpose(dst[:, P * e:P * e + P], flatA[:, COUPLES * e + c::HALF], ident_sb[:])
                            pe.transpose(dst[:, 2 * P:3 * P], flatB[:, c::COUPLES], ident_sb[:]
                                         ).then_inc(t_ready, 1)
                        else:
                            pe.wait_ge(t_taken, n0 * 32 + c + 1 + TBANK_AHEAD)
                            pe.wait_ge(o_taken, n0 * 32 + c - 1 + OBANK_AHEAD)
                            pe.matmul(psO[c % 2], inv_sb[:], tring[:, c % TRING, :], start=True, stop=True
                                      ).then_inc(inv_ready, 1)

                def emit(kind, b, t):
                    if kind == "begin":
                        return
                    for par in range(2):
                        n = tile(b, t, par)
                        for u in range(PARTS):
                            pe_mix(pe, n, u, TILES)
                            if kind != "first" or par == 1:
                                after(u, n[0] - 1, 1 - par, (n[0] + TILES) * 16 + EVAC_AHEAD)
                images(pe, emit)
                for u in range(PARTS):
                    after(u, TILES - 1, 1, 2 * TILES * 16 + EVAC_AHEAD)

            @block.vector
            def _(dve):
                k = Count()

                def link(ins):
                    ins.then_inc(step, 1)
                    dve.wait_ge(step, BATCH * LINKS0 + k.next())
                mean, var = work[:, 0, 0:8], work[:, 1, 0:8]
                mv = work[:, 8:10, 0:8].rearrange("p a b -> p (a b)").rearrange("p (r b m) -> p r b m", r=2, b=BATCH)
                sq = work[:, 10, 0:8]
                for r, (dc, sqs) in enumerate(((dcA, sqA), (dcB, sqB))):
                    for b in range(BATCH):
                        link(dve.bn_aggr(mv[:, r, b, :], dc[:, b * TPB * 6:(b + 1) * TPB * 6]))
                    link(dve.tensor_reduce(sq[:, BATCH * r:BATCH * (r + 1)],
                                           sqs[:].rearrange("p (b n) -> p b n", b=BATCH), AX.X, ALU.add))
                    link(dve.tensor_scalar(sq[:, BATCH * r:BATCH * (r + 1)], sq[:, BATCH * r:BATCH * (r + 1)],
                                           (1.0 + r) / POS, None, ALU.mult))
                mvf = mv.rearrange("p r b m -> p (r b) m")
                link(dve.tensor_scalar(mean, mvf[:, :, 0], 1.0 / PATCH, None, ALU.mult))
                link(dve.tensor_scalar(var, mvf[:, :, 1], 1.0 / SLOTS, None, ALU.mult))
                link(dve.tensor_tensor(var, var, sq, ALU.add))
                dve.sem_inc(s_dve, 1)
                dve.wait_ge(s_pe, 2 * BATCH + 1)
                d = work[:, 3, 0:8]
                link(dve.tensor_scalar(m1[:].rearrange("p r b -> p (r b)"), psS[:, 0:8], -float(PATCH), None, ALU.mult))
                link(dve.tensor_tensor(d, mean, psS[:, 0:8], ALU.subtract))
                link(dve.tensor_tensor(d, d, d, ALU.mult))
                link(dve.tensor_tensor(work[:, 2, 0:8], d, var, ALU.add))
                dve.sem_inc(s_dve, 1)
                dve.wait_ge(s_pe, 2 * BATCH + 2)
                dve_rstd(dve, link, psS[:, 0:8], 8, r1[:].rearrange("p r b -> p (r b)"), BATCH + 1)
                base = k.n
                assert base == LINKS1, base
                dve_weights(dve, 1)

                def emit(kind, b, t):
                    if kind == "begin":
                        dve.tensor_copy(rcur[:], r1[:, :, bass.ds(b, 1)].rearrange("p r a -> p (r a)"))
                        dve.tensor_copy(mcur[:], m1[:, :, bass.ds(b, 1)].rearrange("p r a -> p (r a)")
                                        ).then_inc(norm_ready, 1)
                        dve.wait_ge(norm_ready, b + BATCH + 1)
                        dve.sem_inc(image_begun, 1)
                        return
                    for par in range(2):
                        n = tile(b, t, par)
                        dve_low(dve, n, 0, TILES)
                        for u in range(PARTS):
                            dve_update(dve, n, u, 0, 1, TILES)
                            if u + 1 < PARTS:
                                dve_low(dve, n, u + 1, TILES)
                            dve_update(dve, n, u, 1, 1, TILES)
                images(dve, emit)


def _constants():
    import numpy as np

    h, w = np.meshgrid(np.arange(PATCH), np.arange(PATCH), indexing="ij")
    rows = []
    for kh, kw in ((0, 0), (4, 0), (0, 4), (4, 4)):
        rows.append(np.cos(2 * np.pi * (kh * h + kw * w) / PATCH).ravel() / PATCH)
    pairs = [(kh, kw) for kh in range(PATCH) for kw in (1, 2, 3)] + [(kh, kw) for kw in (0, 4) for kh in (1, 2, 3)]
    for kh, kw in pairs:
        angle = 2 * np.pi * (kh * h + kw * w) / PATCH
        rows += [np.cos(angle).ravel() * 2 ** 0.5 / PATCH, np.sin(angle).ravel() * 2 ** 0.5 / PATCH]
    basis = np.array(rows)
    fwd = np.zeros((2, SLOTS, SLOTS, 2))
    for a in range(2):
        fwd[a, :, :, a] = basis.T
    fwd = fwd.reshape(P, P).astype(np.float32)
    c_a, c_b = np.arange(P), CA + np.arange(P) % CB
    def same(x, y, value):
        return np.where(x[:, None] // CPG == y[None, :] // CPG, value, 0.0)
    gmats = np.stack([same(c_a, c_a, 1 / CPG), same(c_b, c_a, 0.5 / CPG),
                      same(c_a, c_b, 1 / CPG), same(c_b, c_b, 0.5 / CPG)], axis=1).astype(np.float32)
    row_group = np.arange(P) // (P // GROUPS)
    def to(groups):
        return np.where(row_group[:, None] == groups[None, :], GROUPS / P, 0.0)
    smats = np.stack([to(row_group), to(c_a // CPG), to(c_b // CPG)], axis=1).astype(np.float32)
    return fwd, np.ascontiguousarray(fwd.T), np.eye(P, dtype=np.float32), gmats, smats


def kernel(x, L0_conv_w_proj, L0_conv_fft_filter, L1_conv_w_proj, L1_conv_fft_filter):
    import numpy as np
    import concourse.bacc as bacc
    from concourse.bass_utils import run_bass_kernel_spmd

    x = np.ascontiguousarray(x)
    v = x.reshape(BATCH, CH, TPB, 2, 2, PATCH, 4, 4, 2, PATCH)
    x_patch = np.ascontiguousarray(v.transpose(0, 2, 4, 6, 8, 5, 9, 3, 7, 1)).reshape(TILES, PARTS, P, NEWPAIRS, CH)
    fwd, inv, ident, gmats, smats = _constants()
    w0, w1 = np.ascontiguousarray(L0_conv_w_proj), np.ascontiguousarray(L1_conv_w_proj)
    arrays = {
        "x_stat": x.reshape(BATCH, P, XCOLS), "x_patch": x_patch,
        "w0": w0, "w1": w1, "wt0": np.ascontiguousarray(w0.T), "wt1": np.ascontiguousarray(w1.T),
        "f0": np.ascontiguousarray(L0_conv_fft_filter).reshape(CH, -1),
        "f1": np.ascontiguousarray(L1_conv_fft_filter).reshape(CH, -1),
        "fwd": fwd, "inv": inv, "ident": ident, "gmats": gmats, "smats": smats,
    }
    nc = bacc.Bacc("TRN2", target_bir_lowering=False, num_devices=1)
    args = [nc.dram_tensor(n, a.shape, mybir.dt.from_np(a.dtype), kind="ExternalInput").ap() for n, a in arrays.items()]
    out = nc.dram_tensor("out", (TILES, PARTS, P, 4, 2 * CH), F32, kind="ExternalOutput").ap()
    build(nc, *args, out)
    r = run_bass_kernel_spmd(nc, [arrays], core_ids=[0])
    got = r.results[0]["out"]
    got = got.reshape(BATCH, TPB, 4, 2, 2, PATCH, PATCH, 2, 2, 2 * CH)
    y = np.empty((BATCH, CH, TPB, 2, 2, PATCH, 4, 2, 2, 2, PATCH), got.dtype)
    y[:, :CA] = got[..., :2 * CA].reshape(*got.shape[:-1], 2, CA).transpose(0, 10, 1, 4, 9, 5, 2, 3, 7, 8, 6)
    y[:, CA:] = got[..., 2 * CA:].reshape(*got.shape[:-1], 2, CB).transpose(0, 10, 1, 9, 4, 5, 2, 3, 7, 8, 6)
    return y.reshape(BATCH, CH, HEIGHT, WIDTH)
```

```python
from contextlib import ExitStack

import concourse.bass as bass
from concourse import mybir

F32 = mybir.dt.float32
F16 = mybir.dt.float16
ALU = mybir.AluOpType
ACT = mybir.ActivationFunctionType
AX = mybir.AxisListType

BATCH, CH, HEIGHT, WIDTH = 4, 192, 256, 256
P = 128
CA, CB = 128, CH - 128
PATCH = 8
SLOTS = PATCH * PATCH
TILE = 128
HALF = TILE // 2
TPB = (HEIGHT // PATCH) * (WIDTH // PATCH) // TILE
TILES = BATCH * TPB
PARTS = 8
SPP = SLOTS // PARTS
UNITS = 2 * PARTS
UNIT = SPP // 2
SINGLES, PAIRS = 4, 30
FREQS = SINGLES + PAIRS
GROUPS = 32
CPG = CH // GROUPS
POS = HEIGHT * WIDTH
STAT_CHUNK = 1536
BN = 512
XCOLS = CH * POS // P
CHUNKS = XCOLS // STAT_CHUNK
BNPC = STAT_CHUNK // BN
CPT = CHUNKS // TPB
EPS = 1e-5
XSCALE = 8.0
WSCALE = 256.0
TINY = 1e-30
NEWPAIRS = 8
CONSTS = 15
PREP_STEPS = 30
LINKS0, LINKS1 = 13, 27
COUPLES = TILE // 4
TRING = 16

MIX_AHEAD = 4
EVAC_AHEAD = 2
STAT_AHEAD = 2
SQ_AHEAD = 1
INV_AHEAD = TRING
TBANK_AHEAD = 2
OBANK_AHEAD = 2


def build(nc, x_stat, x_patch, w0, w1, wt0, wt1, f0, f1, fwd, inv, ident, gmats, smats, out):
    x1a = nc.dram_tensor("x1a_scratch", (TILES, PARTS, P, SPP * TILE), F32, kind="Internal").ap()
    x1b = nc.dram_tensor("x1b_scratch", (TILES, PARTS, P, SPP * HALF), F32, kind="Internal").ap()
    gn_dram = nc.dram_tensor("gn_scratch", (2, CH, FREQS), F32, kind="Internal").ap()

    ctx = ExitStack()
    with ctx:
        def sb(name, shape, dt=F32):
            return ctx.enter_context(nc.sbuf_tensor(name, shape, dt))

        def sem(name):
            return ctx.enter_context(nc.semaphore(name))

        XA = [sb(f"XA{i}", [P, SLOTS, TILE]) for i in range(2)]
        XB = [sb(f"XB{i}", [P, SLOTS, HALF]) for i in range(2)]
        WA = sb("WA", [P, FREQS, 2, CH], F16)
        WB = sb("WB", [P, FREQS, 2, CH], F16)
        highA = sb("highA", [P, 2, SPP, TILE], F16)
        lowA = sb("lowA", [P, 2, SPP, TILE], F16)
        splitB = sb("splitB", [P, 2, SPP, TILE], F16)
        NX = 4
        XIN = NEWPAIRS * CH
        arena = sb("arena", [P, NX * XIN + 2 * STAT_CHUNK])
        xin = arena[:, 0:NX * XIN].rearrange("p (s q c) -> p s q c", s=NX, q=NEWPAIRS)
        statin = arena[:, NX * XIN:NX * XIN + 2 * STAT_CHUNK].rearrange("p (s n) -> p s n", s=2)
        COUPLE = 2 * CH
        tring = arena[:, 0:TRING * COUPLE].rearrange("p (s n) -> p s n", s=TRING)
        oring = arena[:, TRING * COUPLE:(TRING + 8) * COUPLE].rearrange("p (s j n) -> p s j n", s=2, j=4)

        fwd_sb = sb("fwd_sb", [P, P])
        inv_sb = sb("inv_sb", [P, P])
        ident_sb = fwd_sb
        gm = sb("gm", [P, 4, P])
        sm = gm[:, 0:3, :]
        bn = sb("bn", [P, CPT * BNPC * 6])
        fold = sb("fold", [P, 2])
        folded = sb("folded", [P, TPB, 3])
        junk = sb("junk", [P, SPP * TILE + SPP * HALF], F16)
        junkA = junk[:, 0:SPP * TILE].rearrange("p (k n) -> p k n", k=SPP)
        junkB = junk[:, SPP * TILE:].rearrange("p (k n) -> p k n", k=SPP)
        centA = sb("centA", [P, TILE])
        centB = sb("centB", [P, HALF])
        sqA = sb("sqA", [P, TILES * PARTS])
        sqB = sb("sqB", [P, TILES * PARTS])
        dcA = sb("dcA", [P, TILES * 6])
        dcB = sb("dcB", [P, TILES * 6])
        scale = sb("scale", [P, 2, 2])
        rcur = sb("rcur", [P, 2])
        mcur = sb("mcur", [P, 2])
        r1 = sb("r1", [P, 2, TILES])
        m1 = sb("m1", [P, 2, TILES])
        work = sb("work", [P, 12, 2 * BATCH])

        psMA = ctx.enter_context(nc.psum_tensor("psMA", [P, 2, 512], F32))
        psMB = ctx.enter_context(nc.psum_tensor("psMB", [P, 2, 512], F32))
        psC = ctx.enter_context(nc.psum_tensor("psC", [P, 3, 512], F32))
        psS = ctx.enter_context(nc.psum_tensor("psS", [P, 512], F32))
        psFA, psFB = psC[:, 0:2, :], psC[:, 2, :]
        psT = psC[:, 0:2, :]
        psO = [psC[:, 2, 0:COUPLE], psS[:, 0:COUPLE]]

        wnat = XA[0][:, 0:8, :].rearrange("p a b -> p (a b)")[:, 0:4 * CH].rearrange("p (l c) -> p l c", l=4)
        filt = XA[0][:, 8:10, :].rearrange("p a b -> p (a b)")[:, 0:160].rearrange("p (l h w) -> p l h w", l=4, h=PATCH)
        geff = XA[0][:, 10:12, :].rearrange("p a b -> p (a b)")[:, 0:4 * FREQS].rearrange("p (l k) -> p l k", l=4)
        gnorm = XA[0][:, 12:14, :].rearrange("p a b -> p (a b)")[:, 0:4 * FREQS].rearrange("p (l k) -> p l k", l=4)
        KH = FREQS // 2
        gall = XA[1][:, :, :].rearrange("p a b -> p (a b)")[:, 0:CH * FREQS].rearrange("p (o k) -> p k o", k=FREQS)
        def wprod(layer, i):
            flat = (XB[1][:].rearrange("p a b -> p (a b)") if i % 2 == 0 else
                    arena if layer else XB[0][:].rearrange("p a b -> p (a b)"))
            return flat[:, 0:KH * CH].rearrange("p (k o) -> p k o", k=KH)
        wtr = XB[1][:, :, :].rearrange("p a b -> p (a b)")[:, KH * CH:KH * CH + 2 * CH].rearrange("p (r o) -> p r o", r=2)

        const_in = sem("const_in")
        prep = sem("prep")
        gn_out = sem("gn_out")
        w_in = [sem(f"w_in{i}") for i in range(2)]
        w_prod = sem("w_prod")
        w_high = sem("w_high")
        w_low = sem("w_low")
        xin_in = [sem(f"xin_in{i}") for i in range(NX)]
        stat_in = [sem(f"stat_in{i}") for i in range(2)]
        stat_used = sem("stat_used")
        step = sem("step")
        folding = sem("folding")
        s_dve = sem("s_dve")
        s_pe = sem("s_pe")
        s_act = sem("s_act")
        image_begun = sem("image_begun")
        carried = sem("carried")
        norm_ready = sem("norm_ready")
        fwd_ready = sem("fwd_ready")
        fwd_taken = sem("fwd_taken")
        cent = sem("cent")
        high_ready = sem("high_ready")
        low_ready = sem("low_ready")
        mix_ready = sem("mix_ready")
        mix_taken = sem("mix_taken")
        x_out = [sem(f"x_out{i}") for i in range(2)]
        x_free = sem("x_free")
        sq_done = sem("sq_done")
        x_in = [[sem(f"x_in{i}_{u}") for u in range(PARTS)] for i in range(2)]
        t_ready = sem("t_ready")
        t_taken = sem("t_taken")
        inv_ready = sem("inv_ready")
        o_taken = sem("o_taken")
        o_out = [sem(f"o_out{i}") for i in range(2)]
        o_free = sem("o_free")

        def part(t, u):
            return t[:, SPP * u:SPP * (u + 1), :]

        def norm_of(n, layer):
            if layer == 0:
                return [rcur[:, i:i + 1] for i in range(2)], [mcur[:, i:i + 1] for i in range(2)]
            return ([r1[:, i, bass.ds(n[0], 1)] for i in range(2)], [m1[:, i, bass.ds(n[0], 1)] for i in range(2)])

        def act_high(act, n, u, layer, rows="AB"):
            par, slot = n[1], u % 2
            a, b = part(XA[par], u), part(XB[par], u)
            base = layer * TILES
            r, m = norm_of(n, layer)
            first = 1 if u == 0 else 0
            if "A" in rows:
                act.wait_ge(mix_ready, n[0] * 16 + base * 16 + 2 * u - 2 + MIX_AHEAD)
                if layer == 1:
                    act.wait_ge(x_in[par][u], n[2] * 32 + 32)
                    act.sem_inc(carried, 1)
                if u == 0:
                    act.activation(centA[:], a[:, 0, :], ACT.Identity, bias=m[0])
                    act.activation(centB[:], b[:, 0, :], ACT.Identity, bias=m[1]).then_inc(cent, 1)
                    act.wait_ge(cent, n[0] + base + 1)
                    act.sem_inc(carried, 1)
                    act.activation(highA[:, slot, 0, :], centA[:], ACT.Copy, scale=r[0])
                act.activation(highA[:, slot, first:, :], a[:, first:, :], ACT.Copy, scale=r[0]).then_inc(high_ready, 1)
            if "B" in rows:
                if u == 0:
                    act.activation(splitB[0:64, slot, 0, 0:HALF], centB[0:64, :], ACT.Copy, scale=r[1][0:64])
                    act.activation(splitB[64:P, slot, 0, HALF:TILE], centB[64:P, :], ACT.Copy, scale=r[1][64:P])
                act.activation(splitB[0:64, slot, first:, 0:HALF], b[0:64, first:, :], ACT.Copy, scale=r[1][0:64])
                act.activation(splitB[64:P, slot, first:, HALF:TILE], b[64:P, first:, :], ACT.Copy,
                               scale=r[1][64:P]).then_inc(high_ready, 1)

        def dve_low(dve, n, u, layer, rows="AB"):
            par, slot = n[1], u % 2
            a, b = part(XA[par], u), part(XB[par], u)
            r, _ = norm_of(n, layer)
            done = n[0] * 16 + layer * TILES * 16 + 2 * u

            def low(o, v, r, h):
                return dve.scalar_tensor_tensor(out=o, in0=v, scalar=r, in1=h, op0=ALU.mult, op1=ALU.subtract)
            first = 1 if u == 0 else 0
            if "A" in rows:
                dve.wait_ge(high_ready, done + 1)
                if u == 0:
                    low(lowA[:, slot, 0, :], centA[:], r[0], highA[:, slot, 0, :])
                low(lowA[:, slot, first:, :], a[:, first:, :], r[0], highA[:, slot, first:, :])
            if "B" in rows:
                dve.wait_ge(high_ready, done + 2)
                if u == 0:
                    low(splitB[64:P, slot, 0, 0:HALF], centB[0:64, :], r[1][0:64], splitB[0:64, slot, 0, 0:HALF])
                    low(splitB[0:64, slot, 0, HALF:TILE], centB[64:P, :], r[1][64:P], splitB[64:P, slot, 0, HALF:TILE])
                low(splitB[64:P, slot, first:, 0:HALF], b[0:64, first:, :], r[1][0:64],
                    splitB[0:64, slot, first:, 0:HALF])
                low(splitB[0:64, slot, first:, HALF:TILE], b[64:P, first:, :], r[1][64:P],
                    splitB[64:P, slot, first:, HALF:TILE]).then_inc(low_ready, 1)

        def dve_update(dve, n, u, h, layer, base):
            par, v = n[1], 2 * u + h
            dve.wait_ge(mix_ready, n[0] * 16 + base * 16 + v + 1 + MIX_AHEAD)
            xa = XA[par][:, UNIT * v:UNIT * (v + 1), :].rearrange("p a b -> p (a b)")
            xb = XB[par][:, UNIT * v:UNIT * (v + 1), :].rearrange("p a b -> p (a b)")
            dve.scalar_tensor_tensor(out=xa, in0=psMA[:, h, :], scalar=scale[:, layer, 0:1], in1=xa,
                                     op0=ALU.mult, op1=ALU.add)
            dve.scalar_tensor_tensor(out=xb, in0=psMB[:, h, 0:UNIT * HALF], scalar=scale[:, layer, 1:2], in1=xb,
                                     op0=ALU.mult, op1=ALU.add).then_inc(mix_taken, 1)

        def pe_mix(pe, n, u, base, units=(0, 1)):
            slot = u % 2
            if 0 in units:
                pe.wait_ge(low_ready, n[0] * 8 + base * 8 + u + 1)
            for h in units:
                v = 2 * u + h
                pe.wait_ge(mix_taken, n[0] * 16 + base * 16 + v - 1 + EVAC_AHEAD)
                if v == 0:
                    blocks = [(s, s, 1) for s in range(SINGLES)]
                else:
                    first = SINGLES + 2 * (v - 1)
                    blocks = [(first, 0, 2), (first + 1, 2, 2)]
                for w, s, m in blocks:
                    src = slice(UNIT * h + s, UNIT * h + s + m)
                    ins = [(WA[:, w, 0, :], highA), (WA[:, w, 1, :], highA), (WA[:, w, 0, :], lowA),
                           (WB[:, w, 0, :], splitB), (WB[:, w, 1, :], splitB)]
                    for i, (wt, xs) in enumerate(ins):
                        pe.matmul(psMA[:, h, s * TILE:(s + m) * TILE], wt[:, 0:CA], xs[:, slot, src, :],
                                  start=(i == 0), stop=(i == len(ins) - 1))
                for w, s, m in blocks:
                    src = slice(UNIT * h + s, UNIT * h + s + m)
                    ins = [(WA[:, w, 0, :], highA), (WA[:, w, 1, :], highA), (WA[:, w, 0, :], lowA),
                           (WB[:, w, 0, :], splitB), (WB[:, w, 1, :], splitB)]
                    for i, (wt, xs) in enumerate(ins):
                        for q in range(2):
                            mm = pe.matmul(psMB[64 * q:64 * q + 64, h, s * HALF:(s + m) * HALF], wt[:, CA:CH],
                                           xs[:, slot, src, HALF * q:HALF * q + HALF],
                                           start=(i == 0), stop=(i == len(ins) - 1))
                mm.then_inc(mix_ready, 1)

        class Count:
            def __init__(self):
                self.n = 0

            def next(self, k=1):
                self.n += k
                return self.n

        def dve_rstd(dve, link, var, n, out_r, act_value):
            ve, root, r, t = (work[:, i, 0:n] for i in (4, 5, 6, 7))
            link(dve.tensor_scalar(ve, var, EPS, None, ALU.add))
            dve.sem_inc(s_dve, 1)
            dve.wait_ge(s_act, act_value)
            link(dve.reciprocal(r, root))
            link(dve.tensor_tensor(t, r, r, ALU.mult))
            link(dve.tensor_tensor(t, t, ve, ALU.mult))
            link(dve.tensor_scalar(t, t, -0.5, 1.5, ALU.mult, ALU.add))
            link(dve.tensor_tensor(t, t, r, ALU.mult))
            link(dve.tensor_scalar(out_r, t, XSCALE, None, ALU.mult))

        def load_weights(eng, layer):
            wt = (wt0, wt1)[layer]
            eng.dma_start(gall.rearrange("p k o -> p o k"),
                          gn_dram[layer:layer + 1].rearrange("a o k -> a (o k)").to_broadcast([P, CH * FREQS])
                          .rearrange("p (o k) -> p o k", k=FREQS)).then_inc(w_in[layer], 16)
            eng.dma_start(wtr[:, 0, :], wt[0:CA, :]).then_inc(w_in[layer], 16)
            eng.dma_start(wtr[0:CB, 1, :], wt[CA:CH, :]).then_inc(w_in[layer], 16)
            eng.dma_start(wtr[CB:P, 1, :], wt[CA:CH, :]).then_inc(w_in[layer], 16)

        def w_block(i):
            return i // 2, slice(KH * (i % 2), KH * (i % 2) + KH)

        def dve_product(dve, layer, i):
            rows, ks = w_block(i)
            if i == 0:
                dve.wait_ge(w_in[layer], 64)
            if i >= 2:
                dve.wait_ge(w_low, 4 * layer + i - 1)
            w = wtr[:, rows, :].rearrange("p (a o) -> p a o", a=1).to_broadcast([P, KH, CH])
            dve.tensor_tensor(wprod(layer, i), gall[:, ks, :], w, ALU.mult).then_inc(w_prod, 1)

        def dve_weight_low(dve, layer, i):
            rows, ks = w_block(i)
            dve.wait_ge(w_high, 4 * layer + i + 1)
            W = (WA, WB)[rows]
            dve.tensor_tensor(W[:, ks, 1, :], wprod(layer, i), W[:, ks, 0, :], ALU.subtract).then_inc(w_low, 1)

        def act_weights(act, layer):
            for i in range(4):
                rows, ks = w_block(i)
                act.wait_ge(w_prod, 4 * layer + i + 1)
                act.copy((WA, WB)[rows][:, ks, 0, :], wprod(layer, i)).then_inc(w_high, 1)

        with nc.Block() as block:
            def pairs(eng, emit):
                with eng.Fori(0, BATCH - 1) as b:
                    emit("begin", b, None)
                    with eng.Fori(0, TPB // 2 - 1) as t:
                        emit("stat", b, t)
                    emit("stat end", b, TPB // 2 - 1)
                emit("begin", BATCH - 1, None)
                with eng.Fori(0, TPB // 2 - 1) as t:
                    emit("plain", BATCH - 1, t)
                emit("plain end", BATCH - 1, TPB // 2 - 1)

            def more(kind, par):
                return kind != "plain end" or par == 0

            def leads(kind, par):
                return not kind.endswith("end") or par == 0

            def next_tile(b, t, par):
                return tile(b, t, 1) if par == 0 else (b * TPB + t * 2 + 2, 0, b * (TPB // 2) + t + 1)

            def stat_chunks(kind, u):
                return [] if kind.startswith("plain") else [(0, 1), (2,), (3,), (4,), (5,), (6,), (7,), ()][u]

            def tile(b, t, par):
                return (b * TPB + t * 2 + par, par, b * (TPB // 2) + t)

            @block.sync
            def _(sp):
                def load_stat(image, chunk, s):
                    sp.dma_start(statin[:, s, :], x_stat[bass.ds(image, 1), :, bass.ds(chunk * STAT_CHUNK, STAT_CHUNK)]
                                 .rearrange("a p n -> (a p) n")).then_inc(stat_in[s], 16)
                for i, w in enumerate((w0, w1)):
                    sp.dma_start(wnat[:, 2 * i, :], w[0:CA, :]).then_inc(const_in, 16)
                    sp.dma_start(wnat[0:CB, 2 * i + 1, :], w[CA:CH, :]).then_inc(const_in, 16)
                    sp.dma_start(wnat[CB:P, 2 * i + 1, :], w[CA:CH, :]).then_inc(const_in, 16)
                for i, f in enumerate((f0, f1)):
                    fv = f.rearrange("o (h w) -> o h w", h=PATCH)
                    sp.dma_start(filt[:, 2 * i, :, :], fv[0:CA]).then_inc(const_in, 16)
                    sp.dma_start(filt[0:CB, 2 * i + 1, :, :], fv[CA:CH]).then_inc(const_in, 16)
                    sp.dma_start(filt[CB:P, 2 * i + 1, :, :], fv[CA:CH]).then_inc(const_in, 16)
                sp.dma_start(fwd_sb[:], fwd).then_inc(const_in, 16)
                sp.dma_start(inv_sb[:], inv).then_inc(const_in, 16)
                sp.dma_start(sm, smats).then_inc(const_in, 16)
                for g in range(NX):
                    sp.dma_start(xin[:, g], x_patch[0, g]).then_inc(xin_in[g], 16)
                with sp.Fori(0, CHUNKS // 2) as c:
                    for s in range(2):
                        sp.wait_ge(stat_used, c * 2 + s - 1 + STAT_AHEAD)
                        load_stat(0, c * 2 + s, s)
                for g in range(NX, PARTS + NX):
                    sp.wait_ge(fwd_ready, 3 * (g - NX) + 3)
                    sp.dma_start(xin[:, g % NX], x_patch[g // PARTS, g % PARTS]).then_inc(xin_in[g % NX], 16)

                def emit(kind, b, t):
                    if kind == "begin":
                        return
                    for par in range(2):
                        n = tile(b, t, par)
                        for u in range(PARTS):
                            for c in stat_chunks(kind, u):
                                chunk = b * CHUNKS + t * 16 + par * 8 + c
                                sp.wait_ge(stat_used, chunk + CHUNKS - 1 + STAT_AHEAD)
                                load_stat(b + 1, t * 16 + par * 8 + c, c % 2)
                            ahead = u + NX
                            if kind != "plain end" or (par == 0 and ahead < PARTS):
                                sp.wait_ge(fwd_ready, n[0] * 24 + 24 + 3 * u + 3)
                                sp.dma_start(xin[:, u % NX],
                                             x_patch[bass.ds(n[0] + 1 + ahead // PARTS, 1), ahead % PARTS]
                                             .rearrange("a p q c -> (a p) q c")).then_inc(xin_in[u % NX], 16)
                            sp.wait_ge(mix_taken, n[0] * 16 + 2 * u + 2 + EVAC_AHEAD)
                            sp.dma_start(x1a[bass.ds(n[0], 1), u].rearrange("a p n -> (a p) n"),
                                         part(XA[par], u).rearrange("p a b -> p (a b)")).then_inc(x_out[par], 16)
                            sp.dma_start(x1b[bass.ds(n[0], 1), u].rearrange("a p n -> (a p) n"),
                                         part(XB[par], u).rearrange("p a b -> p (a b)")).then_inc(x_out[par], 16)
                pairs(sp, emit)
                for par in range(2):
                    sp.wait_ge(x_out[par], TILES // 2 * PARTS * 32)

            @block.gpsimd
            def _(pool):
                pool.wait_ge(prep, PREP_STEPS)
                for i in range(2):
                    pool.dma_start(gn_dram[i, 0:CA, :], gnorm[:, 2 * i, :]).then_inc(gn_out, 16)
                    pool.dma_start(gn_dram[i, CA:CH, :], gnorm[0:CB, 2 * i + 1, :]).then_inc(gn_out, 16)
                pool.wait_ge(gn_out, 64)
                load_weights(pool, 0)
                pool.sem_inc(x_free, 1)
                with pool.Fori(0, TILES // 2) as i:
                    for par in range(2):
                        pool.wait_ge(x_out[par], i * (PARTS * 32) + PARTS * 32)
                        pool.sem_inc(x_free, 1)

            @block.scalar
            def _(act):
                act.sem_inc(sq_done, SQ_AHEAD)
                act_weights(act, 0)

                def take_fwd(par, u, base):
                    for h in range(2):
                        act.wait_ge(fwd_ready, base + 3 * u + 1 + h)
                        act.copy(XA[par][:, :, HALF * h + 8 * u:HALF * h + 8 * u + 8]
                                 .rearrange("p k (q a) -> p k q a", a=2),
                                 psFA[:, h, :].rearrange("p (q k a) -> p k q a", q=4, a=2)).then_inc(fwd_taken, 1)
                    act.wait_ge(fwd_ready, base + 3 * u + 3)
                    act.copy(XB[par][:, :, 8 * u:8 * u + 8].rearrange("p k (q a) -> p k q a", a=2),
                             psFB.rearrange("p (q k a) -> p k q a", q=4, a=2)).then_inc(fwd_taken, 1)

                act.wait_ge(w_low, 4)
                for u in range(PARTS):
                    take_fwd(0, u, 0)

                def squares(n, u):
                    par = n[1]
                    act.wait_ge(mix_taken, n[0] * 16 + 2 * u + 2 + EVAC_AHEAD)
                    act.wait_ge(sq_done, n[0] * 8 + u + SQ_AHEAD)
                    act.sem_inc(carried, 1)
                    first = 1 if u == 0 else 0
                    act.activation(junkA[:, first:, :], part(XA[par], u)[:, first:, :], ACT.Square,
                                   accum_out=sqA[:, bass.ds(n[0] * 8 + u, 1)])
                    act.activation(junkB[:, first:, :], part(XB[par], u)[:, first:, :], ACT.Square,
                                   accum_out=sqB[:, bass.ds(n[0] * 8 + u, 1)]).then_inc(sq_done, 1)

                def emit(kind, b, t):
                    if kind == "begin":
                        act.wait_ge(s_dve, b * 3 + 3)
                        act.activation(work[:, 5, 0:2], work[:, 4, 0:2], ACT.Sqrt).then_inc(s_act, 1)
                        act.wait_ge(norm_ready, b + 1)
                        act.wait_ge(fwd_taken, b * (TPB * 24) + 24)
                        act_high(act, tile(b, 0, 0), 0, 0)
                        return
                    for par in range(2):
                        n = tile(b, t, par)
                        for u in range(PARTS):
                            if u + 1 < PARTS:
                                act_high(act, n, u + 1, 0)
                            if par == 1 and u == 0:
                                squares(tile(b, t, 0), PARTS - 1)
                            if more(kind, par):
                                if u == 0:
                                    act.wait_ge(x_free, n[0] + 1)
                                    act.wait_ge(sq_done, n[0] * 8 + SQ_AHEAD)
                                take_fwd(1 - par, u, n[0] * 24 + 24)
                            if u == PARTS - 1 and leads(kind, par):
                                act.wait_ge(fwd_taken, n[0] * 24 + 48)
                                act_high(act, next_tile(b, t, par), 0, 0)
                            if u >= 1:
                                squares(n, u - 1)
                        if par == 1:
                            squares(n, PARTS - 1)
                pairs(act, emit)

            @block.tensor
            def _(pe):
                pe.sem_inc(mix_ready, MIX_AHEAD)
                pe.wait_ge(const_in, 16 * CONSTS)

                def forward(u, base, loads, first=False):
                    pe.wait_ge(xin_in[u % NX], loads + 16 * (u // NX) + 16)
                    src = xin[:, u % NX]
                    for h in range(2):
                        if not (first and u == 0):
                            pe.wait_ge(fwd_taken, base + 3 * (u - 1) + 1 + h)
                        for q in range(4):
                            mm = pe.matmul(psFA[:, h, q * P:(q + 1) * P], src[:, 4 * h + q, 0:CA], fwd_sb[:],
                                           start=True, stop=True)
                        mm.then_inc(fwd_ready, 1)
                    if not (first and u == 0):
                        pe.wait_ge(fwd_taken, base + 3 * u)
                    for q in range(4):
                        for h in range(2):
                            mm = pe.matmul(psFB[64 * h:64 * h + 64, q * P:(q + 1) * P], src[:, 4 * h + q, CA:CH],
                                           fwd_sb[:], start=True, stop=True)
                    mm.then_inc(fwd_ready, 1)

                for u in range(PARTS):
                    forward(u, 0, 0, first=True)

                def emit(kind, b, t):
                    if kind == "begin":
                        pe.wait_ge(s_dve, b * 3 + 1)
                        pe.matmul(psS[:, 0:1], sm[:, 0, :], work[:, 0, 0:1], start=True, stop=True).then_inc(s_pe, 1)
                        pe.wait_ge(s_dve, b * 3 + 2)
                        pe.matmul(psS[:, 0:2], sm[:, 1, :], work[:, 2, 0:2], start=True, stop=True)
                        pe.matmul(psS[:, 2:4], sm[:, 2, :], work[:, 2, 0:2], start=True, stop=True).then_inc(s_pe, 1)
                        return
                    for par in range(2):
                        n = tile(b, t, par)
                        for u in range(PARTS):
                            if more(kind, par):
                                forward(u, n[0] * 24 + 24, n[0] * 32 + 32)
                            pe_mix(pe, n, u, 0)
                pairs(pe, emit)

            @block.vector
            def _(dve):
                dve.sem_inc(mix_taken, EVAC_AHEAD)
                dve.sem_inc(stat_used, STAT_AHEAD)
                dve.wait_ge(const_in, 16 * CONSTS)
                cnt = Count()

                def pl(ins):
                    ins.then_inc(prep, 1)
                    dve.wait_ge(prep, cnt.next())
                flat = filt.rearrange("p l h w -> p l (h w)")
                pl(dve.tensor_copy(geff[:, :, 0:2], flat[:, :, 0:21:20]))
                pl(dve.tensor_copy(geff[:, :, 2:4], flat[:, :, 4:25:20]))
                for i in range(4):
                    pl(dve.tensor_copy(geff[:, i, 4:28].rearrange("p (h w) -> p h w", w=3), filt[:, i, :, 1:4]))
                for j, kw in enumerate((0, 4)):
                    for kh in (1, 2, 3):
                        pl(dve.tensor_tensor(geff[:, :, 27 + 3 * j + kh], filt[:, :, kh, kw], filt[:, :, 8 - kh, kw],
                                             ALU.add))
                pl(dve.tensor_scalar(geff[:, :, 28:34], geff[:, :, 28:34], 0.5, None, ALU.mult))
                pl(dve.tensor_reduce(work[:, 0, 0:4], wnat, AX.X, ALU.max))
                pl(dve.tensor_reduce(work[:, 1, 0:4], wnat, AX.X, ALU.min))
                pl(dve.tensor_reduce(work[:, 2, 0:4], geff, AX.X, ALU.max))
                pl(dve.tensor_reduce(work[:, 3, 0:4], geff, AX.X, ALU.min))
                pl(dve.tensor_scalar(work[:, 1, 0:4], work[:, 1, 0:4], -1.0, None, ALU.mult))
                pl(dve.tensor_scalar(work[:, 3, 0:4], work[:, 3, 0:4], -1.0, None, ALU.mult))
                pl(dve.tensor_tensor(work[:, 0, 0:4], work[:, 0, 0:4], work[:, 1, 0:4], ALU.max))
                pl(dve.tensor_tensor(work[:, 2, 0:4], work[:, 2, 0:4], work[:, 3, 0:4], ALU.max))
                pl(dve.tensor_tensor(work[:, 0, 0:4], work[:, 0, 0:4], work[:, 2, 0:4], ALU.mult))
                pl(dve.tensor_scalar(work[:, 0, 0:4], work[:, 0, 0:4], TINY, None, ALU.max))
                pl(dve.tensor_scalar(scale[:].rearrange("p l r -> p (l r)"), work[:, 0, 0:4], 1.0 / (XSCALE * WSCALE),
                                     None, ALU.mult))
                pl(dve.reciprocal(work[:, 1, 0:4], work[:, 0, 0:4]))
                pl(dve.tensor_scalar(work[:, 1, 0:4], work[:, 1, 0:4], WSCALE, None, ALU.mult))
                for i in range(4):
                    pl(dve.tensor_scalar(gnorm[:, i, :], geff[:, i, :], work[:, 1, i:i + 1], None, ALU.mult))
                assert cnt.n == PREP_STEPS

                def stats(c, landed):
                    dve.wait_ge(stat_in[c % 2], landed)
                    for j in range(BNPC):
                        i = BNPC * c + j
                        ins = dve.bn_stats(bn[:, 6 * i:6 * i + 6], statin[:, c % 2, BN * j:BN * (j + 1)])
                    ins.then_inc(stat_used, 1)

                def fold_stats(f, t):
                    dve.wait_ge(stat_used, f * CPT + CPT + STAT_AHEAD)
                    dve.sem_inc(image_begun, 1)
                    dve.bn_aggr(fold[:], bn[:]).then_inc(folding, 1)
                    dve.wait_ge(folding, f * 3 + 1)
                    row = folded[:, bass.ds(t, 1), :].rearrange("p a m -> p (a m)")
                    dve.tensor_copy(row[:, 1:2], fold[:, 0:1]).then_inc(folding, 1)
                    dve.tensor_scalar(row[:, 2:3], fold[:, 1:2], float(CPT * STAT_CHUNK), None, ALU.mult
                                      ).then_inc(folding, 1)
                dve.memset(folded[:], float(CPT * STAT_CHUNK)).then_inc(prep, 1)
                dve.wait_ge(prep, PREP_STEPS + 1)
                for i in range(5):
                    if i < 4:
                        dve_product(dve, 0, i)
                    first, last = (0, 1, 3, 5, 7)[i], (1, 3, 5, 7, TPB)[i]
                    with dve.Fori(first, last) as f:
                        for c in range(CPT):
                            stats(c, f * (CPT * 8) + (c // 2) * 16 + 16)
                        fold_stats(f, f)
                    if i < 4:
                        dve_weight_low(dve, 0, i)

                def emit(kind, b, t):
                    if kind == "begin":
                        dve.wait_ge(folding, b * (3 * TPB) + 3 * TPB)
                        dve.sem_inc(image_begun, 1)
                        k = Count()

                        def link(ins):
                            ins.then_inc(step, 1)
                            dve.wait_ge(step, b * LINKS0 + k.next())
                        link(dve.bn_aggr(work[:, 0, 0:2], folded[:].rearrange("p t m -> p (t m)")))
                        dve.sem_inc(s_dve, 1)
                        dve.wait_ge(s_pe, b * 2 + 1)
                        d = work[:, 1, 0:1]
                        link(dve.tensor_tensor(d, work[:, 0, 0:1], psS[:, 0:1], ALU.subtract))
                        link(dve.tensor_copy(work[:, 2, 0:1], work[:, 0, 0:1]))
                        link(dve.scalar_tensor_tensor(out=work[:, 2, 1:2], in0=d, scalar=d, in1=work[:, 0, 1:2],
                                                      op0=ALU.mult, op1=ALU.add))
                        dve.sem_inc(s_dve, 1)
                        dve.wait_ge(s_pe, b * 2 + 2)
                        link(dve.tensor_copy(work[:, 3, 0:4], psS[:, 0:4]))
                        mv = work[:, 3, 0:4].rearrange("p (r m) -> p m r", m=2)
                        link(dve.tensor_scalar(mcur[:], mv[:, 0, :], -float(PATCH), None, ALU.mult))
                        dve_rstd(dve, link, mv[:, 1, :], 2, rcur[:], b + 1)
                        assert k.n == LINKS0, k.n
                        dve.sem_inc(norm_ready, 1)
                        dve_low(dve, tile(b, 0, 0), 0, 0)
                        return
                    for par in range(2):
                        n = tile(b, t, par)
                        for u in range(PARTS):
                            if u + 1 < PARTS:
                                dve_low(dve, n, u + 1, 0)
                            dve_update(dve, n, u, 0, 0, 0)
                            if u == 0:
                                dve.wait_ge(mix_taken, n[0] * 16 + 1 + EVAC_AHEAD)
                                dve.bn_stats(dcA[:, bass.ds(n[0] * 6, 6)], XA[par][:, 0, :])
                                dve.bn_stats(dcB[:, bass.ds(n[0] * 6, 6)], XB[par][:, 0, :])
                            if u == PARTS - 1 and leads(kind, par):
                                dve_low(dve, next_tile(b, t, par), 0, 0)
                            dve_update(dve, n, u, 1, 0, 0)
                            for c in stat_chunks(kind, u):
                                stats(c, (b * CHUNKS + t * 16 + CHUNKS) * 8 + (par * 4 + c // 2) * 16 + 16)
                            if u == PARTS - 2 and kind.startswith("stat"):
                                fold_stats(n[0] + TPB, t * 2 + par)
                pairs(dve, emit)

        with nc.Block() as block:
            def pairs(eng, emit):
                emit("first", 0)
                with eng.Fori(1, TILES // 2 - 1) as t:
                    emit("pair", t)
                emit("last", TILES // 2 - 1)

            def tile(t, par):
                return (t * 2 + par, par, t)

            def order(v):
                def upto(first, last):
                    return max(0, min(COUPLES, (v - first + 1) * COUPLES // (last - first + 1)))

                def before(first, last):
                    return max(0, min(COUPLES, (v - first) * COUPLES // (last - first + 1)))
                ts = [("T", c) for c in range(before(1, 11), upto(1, 11))]
                cs = [("I", c) for c in range(before(2, 15), upto(2, 15))]
                both = []
                while ts or cs:
                    both += ts[:1] + cs[:1]
                    ts, cs = ts[1:], cs[1:]
                return both

            def done(what, v):
                return 1 + max([c for w in range(v + 1) for k, c in order(w) if k == what], default=-1)

            @block.sync
            def _(sp):
                sp.dma_start(ident_sb[:], ident).then_inc(const_in, 16)
                sp.dma_start(gm[:], gmats).then_inc(const_in, 16)
                load_weights(sp, 1)

                def load(n, u, par):
                    sp.dma_start(part(XA[par], u).rearrange("p a b -> p (a b)"),
                                 x1a[bass.ds(n, 1), u].rearrange("a p n -> (a p) n")).then_inc(x_in[par][u], 16)
                    sp.dma_start(part(XB[par], u).rearrange("p a b -> p (a b)"),
                                 x1b[bass.ds(n, 1), u].rearrange("a p n -> (a p) n")).then_inc(x_in[par][u], 16)
                for u in range(PARTS):
                    load(0, u, 0)
                sp.wait_ge(w_low, 8)

                def store(n, g):
                    sp.wait_ge(o_taken, (n[0] - 1) * 32 + 4 * g + 4 + OBANK_AHEAD)
                    sp.dma_start(out[bass.ds(n[0] - 1, 1), g].rearrange("a p j n -> (a p) (j n)"),
                                 oring[:, g % 2].rearrange("p j n -> p (j n)")).then_inc(o_out[g % 2], 16)

                def stores(n, v):
                    for g in range(done("I", v - 1) // 4, done("I", v) // 4):
                        store(n, g)

                def emit(kind, t):
                    for par in range(2):
                        n = tile(t, par)
                        before = kind != "first" or par == 1
                        for v in range(UNITS):
                            if before:
                                for u in {0: (6,), 1: (7,)}.get(v, ()):
                                    load(n[0], u, par)
                                stores(n, v)
                            if v >= 11 and (kind != "last" or par == 0):
                                if before and v == 11:
                                    sp.wait_ge(t_ready, n[0] * 32)
                                for u in {11: (0, 1), 12: (2,), 13: (3,), 14: (4,), 15: (5,)}[v]:
                                    load(n[0] + 1, u, 1 - par)
                pairs(sp, emit)
                for v in range(UNITS):
                    stores((TILES, 0, TILES // 2), v)
                for s in range(2):
                    sp.wait_ge(o_out[s], TILES * PARTS // 2 * 16)

            @block.gpsimd
            def _(pool):
                pool.sem_inc(o_free, 2)
                with pool.Fori(0, TILES * PARTS // 2) as i:
                    for s in range(2):
                        pool.wait_ge(o_out[s], i * 16 + 16)
                        pool.sem_inc(o_free, 1)

            @block.scalar
            def _(act):
                act.sem_inc(t_taken, TBANK_AHEAD)
                act.sem_inc(o_taken, OBANK_AHEAD)
                act.wait_ge(s_dve, 3 * BATCH + 3)
                act.activation(work[:, 5, 0:8], work[:, 4, 0:8], ACT.Sqrt).then_inc(s_act, 1)
                act_weights(act, 1)

                def after(v, before):
                    c0 = before * COUPLES
                    for what, c in order(v):
                        if what == "T":
                            act.wait_ge(t_ready, c0 + c + 1)
                            act.wait_ge(inv_ready, c0 + c + 1 - TRING + INV_AHEAD)
                            act.copy(tring[:, c % TRING, :], psT[:, c % 2, 0:COUPLE]).then_inc(t_taken, 1)
                        else:
                            act.wait_ge(inv_ready, c0 + c + 1 + INV_AHEAD)
                            if c % 4 == 0:
                                act.wait_ge(o_free, before * PARTS + c // 4 + 1)
                            act.copy(oring[:, c // 4 % 2, c % 4, :], psO[c % 2]).then_inc(o_taken, 1)

                def emit(kind, t):
                    if kind == "first":
                        act.wait_ge(norm_ready, BATCH + 1)
                        act_high(act, tile(t, 0), 0, 1)
                    for par in range(2):
                        n = tile(t, par)
                        for u in range(PARTS):
                            for h in range(2):
                                if u + 1 < PARTS:
                                    act_high(act, n, u + 1, 1, "AB"[h])
                                elif kind != "last" or par == 0:
                                    act_high(act, tile(t + par, 1 - par), 0, 1, "AB"[h])
                                if kind != "first" or par == 1:
                                    after(2 * u + h, n[0] - 1)

                pairs(act, emit)
                for v in range(UNITS):
                    after(v, TILES - 1)

            @block.tensor
            def _(pe):
                pe.sem_inc(inv_ready, INV_AHEAD)
                pe.wait_ge(const_in, 16 * (CONSTS + 2))
                for i in range(2):
                    pe.wait_ge(s_dve, 3 * BATCH + 1 + i)
                    src = work[:, (0, 2)[i], 0:8]
                    for j in range(2):
                        pe.matmul(psS[:, BATCH * j:BATCH * (j + 1)], gm[:, 2 * j, :], src[:, 0:BATCH],
                                  start=True, stop=False)
                        mm = pe.matmul(psS[:, BATCH * j:BATCH * (j + 1)], gm[:, 2 * j + 1, :], src[:, BATCH:2 * BATCH],
                                       start=False, stop=True)
                    mm.then_inc(s_pe, 1)
                pe.wait_ge(s_dve, 3 * BATCH + 3)

                def after(v, n0, buf, ready):
                    for what, c in order(v):
                        if what == "T":
                            if c == 0:
                                pe.wait_ge(mix_taken, ready)
                            pe.wait_ge(t_taken, n0 * 32 + c - 1 + TBANK_AHEAD)
                            dst = psT[:, c % 2, :]
                            flatA = XA[buf][:].rearrange("p k n -> p (k n)")
                            flatB = XB[buf][:].rearrange("p k n -> p (k n)")
                            for e in range(2):
                                pe.transpose(dst[:, P * e:P * e + P], flatA[:, COUPLES * e + c::HALF], ident_sb[:])
                            pe.transpose(dst[:, 2 * P:3 * P], flatB[:, c::COUPLES], ident_sb[:]
                                         ).then_inc(t_ready, 1)
                        else:
                            pe.wait_ge(t_taken, n0 * 32 + c + 1 + TBANK_AHEAD)
                            pe.wait_ge(o_taken, n0 * 32 + c - 1 + OBANK_AHEAD)
                            pe.matmul(psO[c % 2], inv_sb[:], tring[:, c % TRING, :], start=True, stop=True
                                      ).then_inc(inv_ready, 1)

                def emit(kind, t):
                    for par in range(2):
                        n = tile(t, par)
                        for u in range(PARTS):
                            for h in range(2):
                                pe_mix(pe, n, u, TILES, (h,))
                                if kind != "first" or par == 1:
                                    after(2 * u + h, n[0] - 1, 1 - par, (n[0] + TILES) * 16 + EVAC_AHEAD)
                pairs(pe, emit)
                for v in range(UNITS):
                    after(v, TILES - 1, 1, 2 * TILES * 16 + EVAC_AHEAD)

            @block.vector
            def _(dve):
                k = Count()

                def link(ins):
                    ins.then_inc(step, 1)
                    dve.wait_ge(step, BATCH * LINKS0 + k.next())
                mean, var = work[:, 0, 0:8], work[:, 1, 0:8]
                mv = work[:, 8:10, 0:8].rearrange("p a b -> p (a b)").rearrange("p (r b m) -> p r b m", r=2, b=BATCH)
                sq = work[:, 10, 0:8]
                for r, (dc, sqs) in enumerate(((dcA, sqA), (dcB, sqB))):
                    for b in range(BATCH):
                        link(dve.bn_aggr(mv[:, r, b, :], dc[:, b * TPB * 6:(b + 1) * TPB * 6]))
                    link(dve.tensor_reduce(sq[:, BATCH * r:BATCH * (r + 1)],
                                           sqs[:].rearrange("p (b n) -> p b n", b=BATCH), AX.X, ALU.add))
                    link(dve.tensor_scalar(sq[:, BATCH * r:BATCH * (r + 1)], sq[:, BATCH * r:BATCH * (r + 1)],
                                           (1.0 + r) / POS, None, ALU.mult))
                mvf = mv.rearrange("p r b m -> p (r b) m")
                link(dve.tensor_scalar(mean, mvf[:, :, 0], 1.0 / PATCH, None, ALU.mult))
                link(dve.tensor_scalar(var, mvf[:, :, 1], 1.0 / SLOTS, None, ALU.mult))
                link(dve.tensor_tensor(var, var, sq, ALU.add))
                dve.sem_inc(s_dve, 1)
                dve.wait_ge(s_pe, 2 * BATCH + 1)
                d = work[:, 3, 0:8]
                by_tile = "p r (b t) -> p (r b) t"
                link(dve.tensor_scalar(m1[:].rearrange(by_tile, b=BATCH),
                                       psS[:, 0:8].rearrange("p (n a) -> p n a", a=1).to_broadcast([P, 2 * BATCH, TPB]),
                                       -float(PATCH), None, ALU.mult))
                link(dve.tensor_tensor(d, mean, psS[:, 0:8], ALU.subtract))
                link(dve.tensor_tensor(d, d, d, ALU.mult))
                link(dve.tensor_tensor(work[:, 2, 0:8], d, var, ALU.add))
                dve.sem_inc(s_dve, 1)
                dve.wait_ge(s_pe, 2 * BATCH + 2)
                dve_rstd(dve, link, psS[:, 0:8], 8, work[:, 11, 0:8], BATCH + 1)
                link(dve.tensor_copy(r1[:].rearrange(by_tile, b=BATCH), work[:, 11, 0:8].rearrange("p (n a) -> p n a", a=1)
                                     .to_broadcast([P, 2 * BATCH, TPB])))
                assert k.n == LINKS1, k.n
                dve.sem_inc(norm_ready, 1)
                for i in range(5):
                    if i < 4:
                        dve_product(dve, 1, i)
                    if i >= 1:
                        dve_weight_low(dve, 1, i - 1)

                def emit(kind, t):
                    if kind == "first":
                        dve_low(dve, tile(t, 0), 0, 1)
                    for par in range(2):
                        n = tile(t, par)
                        for u in range(PARTS):
                            for h in range(2):
                                if u + 1 < PARTS:
                                    dve_low(dve, n, u + 1, 1, "AB"[h])
                                elif kind != "last" or par == 0:
                                    dve_low(dve, tile(t + par, 1 - par), 0, 1, "AB"[h])
                                dve_update(dve, n, u, h, 1, TILES)
                pairs(dve, emit)


def _constants():
    import numpy as np

    h, w = np.meshgrid(np.arange(PATCH), np.arange(PATCH), indexing="ij")
    rows = []
    for kh, kw in ((0, 0), (4, 0), (0, 4), (4, 4)):
        rows.append(np.cos(2 * np.pi * (kh * h + kw * w) / PATCH).ravel() / PATCH)
    pairs = [(kh, kw) for kh in range(PATCH) for kw in (1, 2, 3)] + [(kh, kw) for kw in (0, 4) for kh in (1, 2, 3)]
    for kh, kw in pairs:
        angle = 2 * np.pi * (kh * h + kw * w) / PATCH
        rows += [np.cos(angle).ravel() * 2 ** 0.5 / PATCH, np.sin(angle).ravel() * 2 ** 0.5 / PATCH]
    basis = np.array(rows)
    fwd = np.zeros((2, SLOTS, SLOTS, 2))
    for a in range(2):
        fwd[a, :, :, a] = basis.T
    fwd = fwd.reshape(P, P).astype(np.float32)
    c_a, c_b = np.arange(P), CA + np.arange(P) % CB
    def same(x, y, value):
        return np.where(x[:, None] // CPG == y[None, :] // CPG, value, 0.0)
    gmats = np.stack([same(c_a, c_a, 1 / CPG), same(c_b, c_a, 0.5 / CPG),
                      same(c_a, c_b, 1 / CPG), same(c_b, c_b, 0.5 / CPG)], axis=1).astype(np.float32)
    row_group = np.arange(P) // (P // GROUPS)
    def to(groups):
        return np.where(row_group[:, None] == groups[None, :], GROUPS / P, 0.0)
    smats = np.stack([to(row_group), to(c_a // CPG), to(c_b // CPG)], axis=1).astype(np.float32)
    return fwd, np.ascontiguousarray(fwd.T), np.eye(P, dtype=np.float32), gmats, smats


def kernel(x, L0_conv_w_proj, L0_conv_fft_filter, L1_conv_w_proj, L1_conv_fft_filter):
    import numpy as np
    import concourse.bacc as bacc
    from concourse.bass_utils import run_bass_kernel_spmd

    x = np.ascontiguousarray(x)
    v = x.reshape(BATCH, CH, TPB, 2, 2, PATCH, 4, 4, 2, PATCH)
    x_patch = np.ascontiguousarray(v.transpose(0, 2, 4, 6, 8, 5, 9, 3, 7, 1)).reshape(TILES, PARTS, P, NEWPAIRS, CH)
    fwd, inv, ident, gmats, smats = _constants()
    w0, w1 = np.ascontiguousarray(L0_conv_w_proj), np.ascontiguousarray(L1_conv_w_proj)
    arrays = {
        "x_stat": x.reshape(BATCH, P, XCOLS), "x_patch": x_patch,
        "w0": w0, "w1": w1, "wt0": np.ascontiguousarray(w0.T), "wt1": np.ascontiguousarray(w1.T),
        "f0": np.ascontiguousarray(L0_conv_fft_filter).reshape(CH, -1),
        "f1": np.ascontiguousarray(L1_conv_fft_filter).reshape(CH, -1),
        "fwd": fwd, "inv": inv, "ident": ident, "gmats": gmats, "smats": smats,
    }
    nc = bacc.Bacc("TRN2", target_bir_lowering=False, num_devices=1)
    args = [nc.dram_tensor(n, a.shape, mybir.dt.from_np(a.dtype), kind="ExternalInput").ap() for n, a in arrays.items()]
    out = nc.dram_tensor("out", (TILES, PARTS, P, 4, 2 * CH), F32, kind="ExternalOutput").ap()
    build(nc, *args, out)
    r = run_bass_kernel_spmd(nc, [arrays], core_ids=[0])
    got = r.results[0]["out"]
    got = got.reshape(BATCH, TPB, 4, 2, 2, PATCH, PATCH, 2, 2, 2 * CH)
    y = np.empty((BATCH, CH, TPB, 2, 2, PATCH, 4, 2, 2, 2, PATCH), got.dtype)
    y[:, :CA] = got[..., :2 * CA].reshape(*got.shape[:-1], 2, CA).transpose(0, 10, 1, 4, 9, 5, 2, 3, 7, 8, 6)
    y[:, CA:] = got[..., 2 * CA:].reshape(*got.shape[:-1], 2, CB).transpose(0, 10, 1, 9, 4, 5, 2, 3, 7, 8, 6)
    return y.reshape(BATCH, CH, HEIGHT, WIDTH)
```

```python
from contextlib import ExitStack

import concourse.bass as bass
from concourse import mybir

F32 = mybir.dt.float32
F16 = mybir.dt.float16
ALU = mybir.AluOpType
ACT = mybir.ActivationFunctionType
AX = mybir.AxisListType

BATCH, CH, HEIGHT, WIDTH = 4, 192, 256, 256
P = 128
CA, CB = 128, CH - 128
PATCH = 8
SLOTS = PATCH * PATCH
TILE = 128
HALF = TILE // 2
TPB = (HEIGHT // PATCH) * (WIDTH // PATCH) // TILE
TILES = BATCH * TPB
PARTS = 8
SPP = SLOTS // PARTS
UNITS = 2 * PARTS
UNIT = SPP // 2
SINGLES, PAIRS = 4, 30
FREQS = SINGLES + PAIRS
GROUPS = 32
CPG = CH // GROUPS
POS = HEIGHT * WIDTH
STAT_CHUNK = 1536
BN = 512
XCOLS = CH * POS // P
CHUNKS = XCOLS // STAT_CHUNK
BNPC = STAT_CHUNK // BN
CPT = CHUNKS // TPB
EARLY = 4
EARLY_CHUNKS = CHUNKS - CPT
EPS = 1e-5
XSCALE = 8.0
WSCALE = 256.0
TINY = 1e-30
NEWPAIRS = 8
CONSTS = 15
PREP_STEPS = 31
LINKS0, LINKS1 = 13, 27
COUPLES = TILE // 4
TRING = 16

MIX_AHEAD = 4
EVAC_AHEAD = 2
STAT_AHEAD = 2
SQ_AHEAD = 1
INV_AHEAD = TRING
TBANK_AHEAD = 2
OBANK_AHEAD = 2


def build(nc, x_stat, x_patch, w0, w1, wt0, wt1, f0, f1, fwd, inv, ident, gmats, smats, out):
    x1a = nc.dram_tensor("x1a_scratch", (TILES, PARTS, P, SPP * TILE), F32, kind="Internal").ap()
    x1b = nc.dram_tensor("x1b_scratch", (TILES, PARTS, P, SPP * HALF), F32, kind="Internal").ap()
    gn_dram = nc.dram_tensor("gn_scratch", (2, CH, FREQS), F32, kind="Internal").ap()

    ctx = ExitStack()
    with ctx:
        def sb(name, shape, dt=F32):
            return ctx.enter_context(nc.sbuf_tensor(name, shape, dt))

        def sem(name):
            return ctx.enter_context(nc.semaphore(name))

        XA = [sb(f"XA{i}", [P, SLOTS, TILE]) for i in range(2)]
        XB = [sb(f"XB{i}", [P, SLOTS, HALF]) for i in range(2)]
        WA = sb("WA", [P, FREQS, 2, CH], F16)
        WB = sb("WB", [P, FREQS, 2, CH], F16)
        highA = sb("highA", [P, 2, SPP, TILE], F16)
        lowA = sb("lowA", [P, 2, SPP, TILE], F16)
        splitB = sb("splitB", [P, 2, SPP, TILE], F16)
        NX = 4
        XIN = NEWPAIRS * CH
        arena = sb("arena", [P, NX * XIN + 2 * STAT_CHUNK])
        xin = arena[:, 0:NX * XIN].rearrange("p (s q c) -> p s q c", s=NX, q=NEWPAIRS)
        statin = arena[:, NX * XIN:NX * XIN + 2 * STAT_CHUNK].rearrange("p (s n) -> p s n", s=2)
        COUPLE = 2 * CH
        tring = arena[:, 0:TRING * COUPLE].rearrange("p (s n) -> p s n", s=TRING)
        oring = arena[:, TRING * COUPLE:(TRING + 8) * COUPLE].rearrange("p (s j n) -> p s j n", s=2, j=4)

        fwd_sb = sb("fwd_sb", [P, P])
        inv_sb = sb("inv_sb", [P, P])
        ident_sb = fwd_sb
        gm = sb("gm", [P, 4, P])
        sm = gm[:, 0:3, :]
        bn = sb("bn", [P, CPT * BNPC * 6])
        fold = sb("fold", [P, 2])
        folded = sb("folded", [P, TPB, 3])
        junk = sb("junk", [P, SPP * TILE + SPP * HALF], F16)
        junkA = junk[:, 0:SPP * TILE].rearrange("p (k n) -> p k n", k=SPP)
        junkB = junk[:, SPP * TILE:].rearrange("p (k n) -> p k n", k=SPP)
        centA = sb("centA", [P, TILE])
        centB = sb("centB", [P, HALF])
        sqA = sb("sqA", [P, TILES * PARTS])
        sqB = sb("sqB", [P, TILES * PARTS])
        dcA = sb("dcA", [P, TILES * 6])
        dcB = sb("dcB", [P, TILES * 6])
        scale = sb("scale", [P, 2, 2])
        rcur = sb("rcur", [P, 2])
        mcur = sb("mcur", [P, 2])
        r1 = sb("r1", [P, 2, TILES])
        m1 = sb("m1", [P, 2, TILES])
        work = sb("work", [P, 12, 2 * BATCH])

        psMA = ctx.enter_context(nc.psum_tensor("psMA", [P, 2, 512], F32))
        psMB = ctx.enter_context(nc.psum_tensor("psMB", [P, 2, 512], F32))
        psC = ctx.enter_context(nc.psum_tensor("psC", [P, 3, 512], F32))
        psS = ctx.enter_context(nc.psum_tensor("psS", [P, 512], F32))
        psFA, psFB = psC[:, 0:2, :], psC[:, 2, :]
        psT = psC[:, 0:2, :]
        psO = [psC[:, 2, 0:COUPLE], psS[:, 0:COUPLE]]

        wnat = XA[0][:, 0:8, :].rearrange("p a b -> p (a b)")[:, 0:4 * CH].rearrange("p (l c) -> p l c", l=4)
        filt = XA[0][:, 8:10, :].rearrange("p a b -> p (a b)")[:, 0:160].rearrange("p (l h w) -> p l h w", l=4, h=PATCH)
        geff = XA[0][:, 10:12, :].rearrange("p a b -> p (a b)")[:, 0:4 * FREQS].rearrange("p (l k) -> p l k", l=4)
        gnorm = XA[0][:, 12:14, :].rearrange("p a b -> p (a b)")[:, 0:4 * FREQS].rearrange("p (l k) -> p l k", l=4)
        KH = FREQS // 2
        lent = XA[0][:, 14:14 + 2 * STAT_CHUNK // TILE, :].rearrange("p a b -> p (a b)").rearrange("p (s n) -> p s n", s=2)
        early = [statin[:, 0, :], statin[:, 1, :], lent[:, 0, :], lent[:, 1, :]]
        gall = [XA[1 - i][:].rearrange("p a b -> p (a b)")[:, 0:CH * FREQS].rearrange("p (o k) -> p k o", k=FREQS)
                for i in range(2)]
        wtr = [XB[1 - i][:].rearrange("p a b -> p (a b)")[:, KH * CH:KH * CH + 2 * CH].rearrange("p (r o) -> p r o", r=2)
               for i in range(2)]

        def wprod(layer, i):
            flat = arena if layer == 1 and i % 2 == 1 else XB[(1 - layer + i) % 2][:].rearrange("p a b -> p (a b)")
            return flat[:, 0:KH * CH].rearrange("p (k o) -> p k o", k=KH)

        const_in = sem("const_in")
        prep = sem("prep")
        gn_out = sem("gn_out")
        w_in = [sem(f"w_in{i}") for i in range(2)]
        w_prod = sem("w_prod")
        w_high = sem("w_high")
        w_low = sem("w_low")
        xin_in = [sem(f"xin_in{i}") for i in range(NX)]
        stat_in = [sem(f"stat_in{i}") for i in range(EARLY)]
        stat_used = sem("stat_used")
        step = sem("step")
        folding = sem("folding")
        s_dve = sem("s_dve")
        s_pe = sem("s_pe")
        s_act = sem("s_act")
        image_begun = sem("image_begun")
        carried = sem("carried")
        norm_ready = sem("norm_ready")
        fwd_ready = sem("fwd_ready")
        fwd_taken = sem("fwd_taken")
        cent = sem("cent")
        high_ready = sem("high_ready")
        low_ready = sem("low_ready")
        mix_ready = sem("mix_ready")
        mix_taken = sem("mix_taken")
        x_out = [sem(f"x_out{i}") for i in range(2)]
        x_free = sem("x_free")
        sq_done = sem("sq_done")
        x_in = [[sem(f"x_in{i}_{u}") for u in range(PARTS)] for i in range(2)]
        t_ready = sem("t_ready")
        t_taken = sem("t_taken")
        inv_ready = sem("inv_ready")
        o_taken = sem("o_taken")
        o_out = [sem(f"o_out{i}") for i in range(2)]
        o_free = sem("o_free")

        def part(t, u):
            return t[:, SPP * u:SPP * (u + 1), :]

        def norm_of(n, layer):
            if layer == 0:
                return [rcur[:, i:i + 1] for i in range(2)], [mcur[:, i:i + 1] for i in range(2)]
            return ([r1[:, i, bass.ds(n[0], 1)] for i in range(2)], [m1[:, i, bass.ds(n[0], 1)] for i in range(2)])

        def act_high(act, n, u, layer, rows="AB"):
            par, slot = n[1], u % 2
            a, b = part(XA[par], u), part(XB[par], u)
            base = layer * TILES
            r, m = norm_of(n, layer)
            first = 1 if u == 0 else 0
            if "A" in rows:
                act.wait_ge(mix_ready, n[0] * 16 + base * 16 + 2 * u - 2 + MIX_AHEAD)
                if layer == 1:
                    act.wait_ge(x_in[par][u], n[2] * 32 + 32)
                    act.sem_inc(carried, 1)
                if u == 0:
                    act.activation(centA[:], a[:, 0, :], ACT.Identity, bias=m[0])
                    act.activation(centB[:], b[:, 0, :], ACT.Identity, bias=m[1]).then_inc(cent, 1)
                    act.wait_ge(cent, n[0] + base + 1)
                    act.sem_inc(carried, 1)
                    act.activation(highA[:, slot, 0, :], centA[:], ACT.Copy, scale=r[0])
                act.activation(highA[:, slot, first:, :], a[:, first:, :], ACT.Copy, scale=r[0]).then_inc(high_ready, 1)
            if "B" in rows:
                if u == 0:
                    act.activation(splitB[0:64, slot, 0, 0:HALF], centB[0:64, :], ACT.Copy, scale=r[1][0:64])
                    act.activation(splitB[64:P, slot, 0, HALF:TILE], centB[64:P, :], ACT.Copy, scale=r[1][64:P])
                act.activation(splitB[0:64, slot, first:, 0:HALF], b[0:64, first:, :], ACT.Copy, scale=r[1][0:64])
                act.activation(splitB[64:P, slot, first:, HALF:TILE], b[64:P, first:, :], ACT.Copy,
                               scale=r[1][64:P]).then_inc(high_ready, 1)

        def dve_low(dve, n, u, layer, rows="AB"):
            par, slot = n[1], u % 2
            a, b = part(XA[par], u), part(XB[par], u)
            r, _ = norm_of(n, layer)
            done = n[0] * 16 + layer * TILES * 16 + 2 * u

            def low(o, v, r, h):
                return dve.scalar_tensor_tensor(out=o, in0=v, scalar=r, in1=h, op0=ALU.mult, op1=ALU.subtract)
            first = 1 if u == 0 else 0
            if "A" in rows:
                dve.wait_ge(high_ready, done + 1)
                if u == 0:
                    low(lowA[:, slot, 0, :], centA[:], r[0], highA[:, slot, 0, :])
                low(lowA[:, slot, first:, :], a[:, first:, :], r[0], highA[:, slot, first:, :])
            if "B" in rows:
                dve.wait_ge(high_ready, done + 2)
                if u == 0:
                    low(splitB[64:P, slot, 0, 0:HALF], centB[0:64, :], r[1][0:64], splitB[0:64, slot, 0, 0:HALF])
                    low(splitB[0:64, slot, 0, HALF:TILE], centB[64:P, :], r[1][64:P], splitB[64:P, slot, 0, HALF:TILE])
                low(splitB[64:P, slot, first:, 0:HALF], b[0:64, first:, :], r[1][0:64],
                    splitB[0:64, slot, first:, 0:HALF])
                low(splitB[0:64, slot, first:, HALF:TILE], b[64:P, first:, :], r[1][64:P],
                    splitB[64:P, slot, first:, HALF:TILE]).then_inc(low_ready, 1)

        def dve_update(dve, n, u, h, layer, base):
            par, v = n[1], 2 * u + h
            dve.wait_ge(mix_ready, n[0] * 16 + base * 16 + v + 1 + MIX_AHEAD)
            xa = XA[par][:, UNIT * v:UNIT * (v + 1), :].rearrange("p a b -> p (a b)")
            xb = XB[par][:, UNIT * v:UNIT * (v + 1), :].rearrange("p a b -> p (a b)")
            dve.scalar_tensor_tensor(out=xa, in0=psMA[:, h, :], scalar=scale[:, layer, 0:1], in1=xa,
                                     op0=ALU.mult, op1=ALU.add)
            dve.scalar_tensor_tensor(out=xb, in0=psMB[:, h, 0:UNIT * HALF], scalar=scale[:, layer, 1:2], in1=xb,
                                     op0=ALU.mult, op1=ALU.add).then_inc(mix_taken, 1)

        def pe_mix(pe, n, u, base, units=(0, 1)):
            slot = u % 2
            if 0 in units:
                pe.wait_ge(low_ready, n[0] * 8 + base * 8 + u + 1)
            for h in units:
                v = 2 * u + h
                pe.wait_ge(mix_taken, n[0] * 16 + base * 16 + v - 1 + EVAC_AHEAD)
                if v == 0:
                    blocks = [(s, s, 1) for s in range(SINGLES)]
                else:
                    first = SINGLES + 2 * (v - 1)
                    blocks = [(first, 0, 2), (first + 1, 2, 2)]
                for w, s, m in blocks:
                    src = slice(UNIT * h + s, UNIT * h + s + m)
                    ins = [(WA[:, w, 0, :], highA), (WA[:, w, 1, :], highA), (WA[:, w, 0, :], lowA),
                           (WB[:, w, 0, :], splitB), (WB[:, w, 1, :], splitB)]
                    for i, (wt, xs) in enumerate(ins):
                        pe.matmul(psMA[:, h, s * TILE:(s + m) * TILE], wt[:, 0:CA], xs[:, slot, src, :],
                                  start=(i == 0), stop=(i == len(ins) - 1))
                for w, s, m in blocks:
                    src = slice(UNIT * h + s, UNIT * h + s + m)
                    ins = [(WA[:, w, 0, :], highA), (WA[:, w, 1, :], highA), (WA[:, w, 0, :], lowA),
                           (WB[:, w, 0, :], splitB), (WB[:, w, 1, :], splitB)]
                    for i, (wt, xs) in enumerate(ins):
                        for q in range(2):
                            mm = pe.matmul(psMB[64 * q:64 * q + 64, h, s * HALF:(s + m) * HALF], wt[:, CA:CH],
                                           xs[:, slot, src, HALF * q:HALF * q + HALF],
                                           start=(i == 0), stop=(i == len(ins) - 1))
                mm.then_inc(mix_ready, 1)

        class Count:
            def __init__(self):
                self.n = 0

            def next(self, k=1):
                self.n += k
                return self.n

        def dve_rstd(dve, link, var, n, out_r, act_value, meanwhile=None):
            ve, root, r, t = (work[:, i, 0:n] for i in (4, 5, 6, 7))
            link(dve.tensor_scalar(ve, var, EPS, None, ALU.add))
            dve.sem_inc(s_dve, 1)
            if meanwhile:
                meanwhile()
            dve.wait_ge(s_act, act_value)
            link(dve.reciprocal(r, root))
            link(dve.tensor_tensor(t, r, r, ALU.mult))
            link(dve.tensor_tensor(t, t, ve, ALU.mult))
            link(dve.tensor_scalar(t, t, -0.5, 1.5, ALU.mult, ALU.add))
            link(dve.tensor_tensor(t, t, r, ALU.mult))
            link(dve.tensor_scalar(out_r, t, XSCALE, None, ALU.mult))

        def load_weights(eng, layer):
            wt = (wt0, wt1)[layer]
            eng.dma_start(gall[layer].rearrange("p k o -> p o k"),
                          gn_dram[layer:layer + 1].rearrange("a o k -> a (o k)").to_broadcast([P, CH * FREQS])
                          .rearrange("p (o k) -> p o k", k=FREQS)).then_inc(w_in[layer], 16)
            eng.dma_start(wtr[layer][:, 0, :], wt[0:CA, :]).then_inc(w_in[layer], 16)
            eng.dma_start(wtr[layer][0:CB, 1, :], wt[CA:CH, :]).then_inc(w_in[layer], 16)
            eng.dma_start(wtr[layer][CB:P, 1, :], wt[CA:CH, :]).then_inc(w_in[layer], 16)

        def w_block(i):
            return i // 2, slice(KH * (i % 2), KH * (i % 2) + KH)

        def dve_product(dve, layer, i):
            rows, ks = w_block(i)
            if i == 0:
                dve.wait_ge(w_in[layer], 64)
            if i >= 2:
                dve.wait_ge(w_low, 4 * layer + i - 1)
            w = wtr[layer][:, rows, :].rearrange("p (a o) -> p a o", a=1).to_broadcast([P, KH, CH])
            dve.tensor_tensor(wprod(layer, i), gall[layer][:, ks, :], w, ALU.mult).then_inc(w_prod, 1)

        def dve_weight_low(dve, layer, i):
            rows, ks = w_block(i)
            dve.wait_ge(w_high, 4 * layer + i + 1)
            W = (WA, WB)[rows]
            dve.tensor_tensor(W[:, ks, 1, :], wprod(layer, i), W[:, ks, 0, :], ALU.subtract).then_inc(w_low, 1)

        def act_weights(act, layer, blocks=range(4)):
            for i in blocks:
                rows, ks = w_block(i)
                act.wait_ge(w_prod, 4 * layer + i + 1)
                act.copy((WA, WB)[rows][:, ks, 0, :], wprod(layer, i)).then_inc(w_high, 1)

        with nc.Block() as block:
            def pairs(eng, emit):
                emit("begin", 0, None)
                with eng.Fori(0, BATCH - 1) as b:
                    with eng.Fori(0, TPB // 2 - 1) as t:
                        emit("stat", b, t)
                    emit("stat end", b, TPB // 2 - 1)
                with eng.Fori(0, TPB // 2 - 1) as t:
                    emit("plain", BATCH - 1, t)
                emit("plain end", BATCH - 1, TPB // 2 - 1)

            def more(kind, par):
                return kind != "plain end" or par == 0

            def new_norm(kind, par, u):
                return kind == "stat end" and par == 1 and u == PARTS - 1

            def next_tile(b, t, par):
                return tile(b, t, 1) if par == 0 else (b * TPB + t * 2 + 2, 0, b * (TPB // 2) + t + 1)

            def stat_chunks(kind, u):
                return [] if kind.startswith("plain") else [(0, 1), (2,), (3,), (4,), (5,), (6,), (7,), ()][u]

            def tile(b, t, par):
                return (b * TPB + t * 2 + par, par, b * (TPB // 2) + t)

            @block.sync
            def _(sp):
                def load_stat(image, chunk, s):
                    sp.dma_start(early[s], x_stat[bass.ds(image, 1), :, bass.ds(chunk * STAT_CHUNK, STAT_CHUNK)]
                                 .rearrange("a p n -> (a p) n")).then_inc(stat_in[s], 16)
                for s in range(EARLY):
                    load_stat(0, s, s)
                for rounds in ((1, 10), (10, EARLY_CHUNKS // EARLY)):
                    with sp.Fori(*rounds) as c:
                        for s in range(EARLY):
                            sp.wait_ge(stat_used, c * EARLY + s + 1 - EARLY + STAT_AHEAD)
                            load_stat(0, c * EARLY + s, s)
                    if rounds[0] == 1:
                        for g in range(NX):
                            sp.dma_start(xin[:, g], x_patch[0, g]).then_inc(xin_in[g], 16)
                for g in range(NX, PARTS + NX):
                    if g < PARTS:
                        for c in range(EARLY_CHUNKS + 2 * (g - NX), EARLY_CHUNKS + 2 * (g - NX) + 2):
                            sp.wait_ge(stat_used, (c - 1 if g > NX else c + 1 - EARLY) + STAT_AHEAD)
                            load_stat(0, c, c % 2)
                    sp.wait_ge(fwd_ready, 3 * (g - NX) + 3)
                    sp.dma_start(xin[:, g % NX], x_patch[g // PARTS, g % PARTS]).then_inc(xin_in[g % NX], 16)

                def emit(kind, b, t):
                    if kind == "begin":
                        return
                    for par in range(2):
                        n = tile(b, t, par)
                        for u in range(PARTS):
                            for c in stat_chunks(kind, u):
                                chunk = b * CHUNKS + t * 16 + par * 8 + c
                                sp.wait_ge(stat_used, chunk + CHUNKS - 1 + STAT_AHEAD)
                                load_stat(b + 1, t * 16 + par * 8 + c, c % 2)
                            ahead = u + NX
                            if kind != "plain end" or (par == 0 and ahead < PARTS):
                                sp.wait_ge(fwd_ready, n[0] * 24 + 24 + 3 * u + 3)
                                sp.dma_start(xin[:, u % NX],
                                             x_patch[bass.ds(n[0] + 1 + ahead // PARTS, 1), ahead % PARTS]
                                             .rearrange("a p q c -> (a p) q c")).then_inc(xin_in[u % NX], 16)
                            sp.wait_ge(mix_taken, n[0] * 16 + 2 * u + 2 + EVAC_AHEAD)
                            sp.dma_start(x1a[bass.ds(n[0], 1), u].rearrange("a p n -> (a p) n"),
                                         part(XA[par], u).rearrange("p a b -> p (a b)")).then_inc(x_out[par], 16)
                            sp.dma_start(x1b[bass.ds(n[0], 1), u].rearrange("a p n -> (a p) n"),
                                         part(XB[par], u).rearrange("p a b -> p (a b)")).then_inc(x_out[par], 16)
                pairs(sp, emit)
                for par in range(2):
                    sp.wait_ge(x_out[par], TILES // 2 * PARTS * 32)

            @block.gpsimd
            def _(pool):
                pool.wait_ge(prep, PREP_STEPS)
                for i in range(2):
                    pool.dma_start(gn_dram[i, 0:CA, :], gnorm[:, 2 * i, :]).then_inc(gn_out, 16)
                    pool.dma_start(gn_dram[i, CA:CH, :], gnorm[0:CB, 2 * i + 1, :]).then_inc(gn_out, 16)
                pool.wait_ge(gn_out, 64)
                load_weights(pool, 0)
                pool.sem_inc(x_free, 1)
                with pool.Fori(0, TILES // 2 - 1) as i:
                    for par in range(2):
                        pool.wait_ge(x_out[par], i * (PARTS * 32) + PARTS * 32)
                        pool.sem_inc(x_free, 1)
                pool.wait_ge(x_out[0], TILES // 2 * (PARTS * 32))
                pool.wait_ge(sq_done, (TILES - 1) * PARTS + SQ_AHEAD)
                load_weights(pool, 1)

            @block.scalar
            def _(act):
                for i, w in enumerate((w0, w1)):
                    act.dma_start(wnat[:, 2 * i, :], w[0:CA, :]).then_inc(const_in, 16)
                    act.dma_start(wnat[0:CB, 2 * i + 1, :], w[CA:CH, :]).then_inc(const_in, 16)
                    act.dma_start(wnat[CB:P, 2 * i + 1, :], w[CA:CH, :]).then_inc(const_in, 16)
                for i, f in enumerate((f0, f1)):
                    fv = f.rearrange("o (h w) -> o h w", h=PATCH)
                    act.dma_start(filt[:, 2 * i, :, :], fv[0:CA]).then_inc(const_in, 16)
                    act.dma_start(filt[0:CB, 2 * i + 1, :, :], fv[CA:CH]).then_inc(const_in, 16)
                    act.dma_start(filt[CB:P, 2 * i + 1, :, :], fv[CA:CH]).then_inc(const_in, 16)
                act.dma_start(fwd_sb[:], fwd).then_inc(const_in, 16)
                act.dma_start(inv_sb[:], inv).then_inc(const_in, 16)
                act.dma_start(sm, smats).then_inc(const_in, 16)
                act.sem_inc(sq_done, SQ_AHEAD)
                act_weights(act, 0)

                def take_fwd(par, u, base):
                    for h in range(2):
                        act.wait_ge(fwd_ready, base + 3 * u + 1 + h)
                        act.copy(XA[par][:, :, HALF * h + 8 * u:HALF * h + 8 * u + 8]
                                 .rearrange("p k (q a) -> p k q a", a=2),
                                 psFA[:, h, :].rearrange("p (q k a) -> p k q a", q=4, a=2)).then_inc(fwd_taken, 1)
                    act.wait_ge(fwd_ready, base + 3 * u + 3)
                    act.copy(XB[par][:, :, 8 * u:8 * u + 8].rearrange("p k (q a) -> p k q a", a=2),
                             psFB.rearrange("p (q k a) -> p k q a", q=4, a=2)).then_inc(fwd_taken, 1)

                act.wait_ge(w_low, 4)
                act.wait_ge(stat_used, EARLY_CHUNKS + STAT_AHEAD)
                for u in range(PARTS):
                    take_fwd(0, u, 0)

                def squares(n, u):
                    par = n[1]
                    act.wait_ge(mix_taken, n[0] * 16 + 2 * u + 2 + EVAC_AHEAD)
                    act.wait_ge(sq_done, n[0] * 8 + u + SQ_AHEAD)
                    act.sem_inc(carried, 1)
                    first = 1 if u == 0 else 0
                    act.activation(junkA[:, first:, :], part(XA[par], u)[:, first:, :], ACT.Square,
                                   accum_out=sqA[:, bass.ds(n[0] * 8 + u, 1)])
                    act.activation(junkB[:, first:, :], part(XB[par], u)[:, first:, :], ACT.Square,
                                   accum_out=sqB[:, bass.ds(n[0] * 8 + u, 1)]).then_inc(sq_done, 1)

                def norm_root(b):
                    act.wait_ge(s_dve, b * 3 + 3)
                    act.activation(work[:, 5, 0:2], work[:, 4, 0:2], ACT.Sqrt).then_inc(s_act, 1)
                    act.wait_ge(norm_ready, b + 1)

                def emit(kind, b, t):
                    if kind == "begin":
                        norm_root(0)
                        act.wait_ge(fwd_taken, b * (TPB * 24) + 24)
                        act_high(act, tile(b, 0, 0), 0, 0)
                        act_high(act, tile(b, 0, 0), 1, 0)
                        return
                    for par in range(2):
                        n = tile(b, t, par)
                        for u in range(PARTS):
                            if 0 < u < PARTS - 1:
                                act_high(act, n, u + 1, 0)
                            if more(kind, par):
                                if u == 0:
                                    act.wait_ge(x_free, n[0] + 1)
                                    act.wait_ge(sq_done, n[0] * 8 + SQ_AHEAD)
                                take_fwd(1 - par, u, n[0] * 24 + 24)
                            if new_norm(kind, par, u):
                                norm_root(b + 1)
                            if u == PARTS - 1 and more(kind, par):
                                act.wait_ge(fwd_taken, n[0] * 24 + 48)
                                act_high(act, next_tile(b, t, par), 0, 0)
                            if u >= 1:
                                squares(n, u - 1)
                            if u == PARTS - 1:
                                if more(kind, par):
                                    act_high(act, next_tile(b, t, par), 1, 0)
                                squares(n, u)
                pairs(act, emit)
                act.wait_ge(mix_ready, TILES * UNITS + MIX_AHEAD)
                act_weights(act, 1, (0, 1))

            @block.tensor
            def _(pe):
                pe.sem_inc(mix_ready, MIX_AHEAD)
                pe.wait_ge(const_in, 16 * CONSTS)

                def forward(u, base, loads, first=False):
                    pe.wait_ge(xin_in[u % NX], loads + 16 * (u // NX) + 16)
                    src = xin[:, u % NX]
                    for h in range(2):
                        if not (first and u == 0):
                            pe.wait_ge(fwd_taken, base + 3 * (u - 1) + 1 + h)
                        for q in range(4):
                            mm = pe.matmul(psFA[:, h, q * P:(q + 1) * P], src[:, 4 * h + q, 0:CA], fwd_sb[:],
                                           start=True, stop=True)
                        mm.then_inc(fwd_ready, 1)
                    if not (first and u == 0):
                        pe.wait_ge(fwd_taken, base + 3 * u)
                    for q in range(4):
                        for h in range(2):
                            mm = pe.matmul(psFB[64 * h:64 * h + 64, q * P:(q + 1) * P], src[:, 4 * h + q, CA:CH],
                                           fwd_sb[:], start=True, stop=True)
                    mm.then_inc(fwd_ready, 1)

                for u in range(PARTS):
                    forward(u, 0, 0, first=True)

                def norm_mean(b):
                    pe.wait_ge(s_dve, b * 3 + 1)
                    pe.matmul(psS[:, 0:1], sm[:, 0, :], work[:, 0, 0:1], start=True, stop=True).then_inc(s_pe, 1)

                def norm_channels(b):
                    pe.wait_ge(s_dve, b * 3 + 2)
                    pe.matmul(psS[:, 0:2], sm[:, 1, :], work[:, 2, 0:2], start=True, stop=True)
                    pe.matmul(psS[:, 2:4], sm[:, 2, :], work[:, 2, 0:2], start=True, stop=True).then_inc(s_pe, 1)

                def emit(kind, b, t):
                    if kind == "begin":
                        norm_mean(0)
                        norm_channels(0)
                        return
                    for par in range(2):
                        n = tile(b, t, par)
                        for u in range(PARTS):
                            if u == 1:
                                pe_mix(pe, n, u, 0)
                            if more(kind, par):
                                forward(u, n[0] * 24 + 24, n[0] * 32 + 32)
                            if new_norm(kind, par, u):
                                norm_mean(b + 1)
                                pe_mix(pe, n, u, 0, (0,))
                                norm_channels(b + 1)
                                pe_mix(pe, n, u, 0, (1,))
                            elif u != 1:
                                pe_mix(pe, n, u, 0)
                pairs(pe, emit)

            @block.vector
            def _(dve):
                dve.sem_inc(mix_taken, EVAC_AHEAD)
                dve.sem_inc(stat_used, STAT_AHEAD)
                def stats(c, s, landed):
                    dve.wait_ge(stat_in[s], landed)
                    for j in range(BNPC):
                        i = BNPC * c + j
                        ins = dve.bn_stats(bn[:, 6 * i:6 * i + 6], early[s][:, BN * j:BN * (j + 1)])
                    ins.then_inc(stat_used, 1)

                def fold_stats(f, t):
                    dve.wait_ge(stat_used, f * CPT + CPT + STAT_AHEAD)
                    dve.sem_inc(image_begun, 1)
                    dve.bn_aggr(fold[:], bn[:]).then_inc(folding, 1)
                    dve.wait_ge(folding, f * 3 + 1)
                    row = folded[:, bass.ds(t, 1), :].rearrange("p a m -> p (a m)")
                    dve.tensor_copy(row[:, 1:2], fold[:, 0:1]).then_inc(folding, 1)
                    dve.tensor_scalar(row[:, 2:3], fold[:, 1:2], float(CPT * STAT_CHUNK), None, ALU.mult
                                      ).then_inc(folding, 1)
                def early_stats(f, first=0, last=CPT):
                    for c in range(first, last):
                        stats(c, c % EARLY, (f * (CPT // EARLY) + c // EARLY) * 16 + 16)
                    if last == CPT:
                        fold_stats(f, f)
                cnt = Count()

                def pl(ins):
                    ins.then_inc(prep, 1)
                    dve.wait_ge(prep, cnt.next())
                pl(dve.memset(folded[:], float(CPT * STAT_CHUNK)))
                with dve.Fori(0, 2) as f:
                    early_stats(f)
                dve.wait_ge(const_in, 16 * CONSTS)
                flat = filt.rearrange("p l h w -> p l (h w)")
                pl(dve.tensor_copy(geff[:, :, 0:2], flat[:, :, 0:21:20]))
                pl(dve.tensor_copy(geff[:, :, 2:4], flat[:, :, 4:25:20]))
                for i in range(4):
                    pl(dve.tensor_copy(geff[:, i, 4:28].rearrange("p (h w) -> p h w", w=3), filt[:, i, :, 1:4]))
                for j, kw in enumerate((0, 4)):
                    for kh in (1, 2, 3):
                        pl(dve.tensor_tensor(geff[:, :, 27 + 3 * j + kh], filt[:, :, kh, kw], filt[:, :, 8 - kh, kw],
                                             ALU.add))
                pl(dve.tensor_scalar(geff[:, :, 28:34], geff[:, :, 28:34], 0.5, None, ALU.mult))
                pl(dve.tensor_reduce(work[:, 0, 0:4], wnat, AX.X, ALU.max))
                pl(dve.tensor_reduce(work[:, 1, 0:4], wnat, AX.X, ALU.min))
                pl(dve.tensor_reduce(work[:, 2, 0:4], geff, AX.X, ALU.max))
                pl(dve.tensor_reduce(work[:, 3, 0:4], geff, AX.X, ALU.min))
                pl(dve.tensor_scalar(work[:, 1, 0:4], work[:, 1, 0:4], -1.0, None, ALU.mult))
                pl(dve.tensor_scalar(work[:, 3, 0:4], work[:, 3, 0:4], -1.0, None, ALU.mult))
                pl(dve.tensor_tensor(work[:, 0, 0:4], work[:, 0, 0:4], work[:, 1, 0:4], ALU.max))
                pl(dve.tensor_tensor(work[:, 2, 0:4], work[:, 2, 0:4], work[:, 3, 0:4], ALU.max))
                pl(dve.tensor_tensor(work[:, 0, 0:4], work[:, 0, 0:4], work[:, 2, 0:4], ALU.mult))
                pl(dve.tensor_scalar(work[:, 0, 0:4], work[:, 0, 0:4], TINY, None, ALU.max))
                pl(dve.tensor_scalar(scale[:].rearrange("p l r -> p (l r)"), work[:, 0, 0:4], 1.0 / (XSCALE * WSCALE),
                                     None, ALU.mult))
                pl(dve.reciprocal(work[:, 1, 0:4], work[:, 0, 0:4]))
                pl(dve.tensor_scalar(work[:, 1, 0:4], work[:, 1, 0:4], WSCALE, None, ALU.mult))
                for i in range(4):
                    pl(dve.tensor_scalar(gnorm[:, i, :], geff[:, i, :], work[:, 1, i:i + 1], None, ALU.mult))
                assert cnt.n == PREP_STEPS

                early_stats(2)
                for i in range(4):
                    dve_product(dve, 0, i)
                    early_stats(3 + i, 0, CPT // 2)
                    dve_weight_low(dve, 0, i)
                    early_stats(3 + i, CPT // 2)
                for c in range(CPT):
                    stats(c, c % 2, (EARLY_CHUNKS // EARLY + c // 2) * 16 + 16)
                fold_stats(TPB - 1, TPB - 1)

                def norm_rows(b, k):
                    link = linked(b, k)
                    dve.wait_ge(folding, b * (3 * TPB))
                    dve.sem_inc(image_begun, 1)
                    link(dve.bn_aggr(work[:, 0, 0:2], folded[:].rearrange("p t m -> p (t m)")))
                    dve.sem_inc(s_dve, 1)
                    dve.wait_ge(s_pe, b * 2 - 1)
                    d = work[:, 1, 0:1]
                    link(dve.tensor_tensor(d, work[:, 0, 0:1], psS[:, 0:1], ALU.subtract))
                    link(dve.tensor_copy(work[:, 2, 0:1], work[:, 0, 0:1]))
                    link(dve.scalar_tensor_tensor(out=work[:, 2, 1:2], in0=d, scalar=d, in1=work[:, 0, 1:2],
                                                  op0=ALU.mult, op1=ALU.add))
                    dve.sem_inc(s_dve, 1)

                def norm_scale(b, k):
                    link = linked(b, k)
                    dve.wait_ge(s_pe, b * 2)
                    link(dve.tensor_copy(work[:, 3, 0:4], psS[:, 0:4]))
                    mv = work[:, 3, 0:4].rearrange("p (r m) -> p m r", m=2)
                    link(dve.tensor_scalar(mcur[:], mv[:, 0, :], -float(PATCH), None, ALU.mult))
                    dve_rstd(dve, link, mv[:, 1, :], 2, rcur[:], b)
                    assert k.n == LINKS0, k.n
                    dve.sem_inc(norm_ready, 1)

                def linked(b, k):
                    def link(ins):
                        ins.then_inc(step, 1)
                        dve.wait_ge(step, (b - 1) * LINKS0 + k.next())
                    return link

                def emit(kind, b, t):
                    if kind == "begin":
                        k = Count()
                        norm_rows(1, k)
                        norm_scale(1, k)
                        dve_low(dve, tile(0, 0, 0), 0, 0)
                        return
                    k = Count()
                    for par in range(2):
                        n = tile(b, t, par)
                        for u in range(PARTS):
                            if u + 1 < PARTS:
                                dve_low(dve, n, u + 1, 0)
                            if new_norm(kind, par, u):
                                norm_rows(b + 2, k)
                            dve_update(dve, n, u, 0, 0, 0)
                            if new_norm(kind, par, u):
                                norm_scale(b + 2, k)
                            if u == 0:
                                dve.wait_ge(mix_taken, n[0] * 16 + 1 + EVAC_AHEAD)
                                dve.bn_stats(dcA[:, bass.ds(n[0] * 6, 6)], XA[par][:, 0, :])
                                dve.bn_stats(dcB[:, bass.ds(n[0] * 6, 6)], XB[par][:, 0, :])
                            if u == PARTS - 1 and more(kind, par):
                                dve_low(dve, next_tile(b, t, par), 0, 0)
                            dve_update(dve, n, u, 1, 0, 0)
                            for c in stat_chunks(kind, u):
                                stats(c, c % 2, (b * (4 * TPB) + t * 8 + EARLY_CHUNKS // EARLY + CPT // 2 + par * 4 + c // 2
                                                 + 1) * 16)
                            if u == PARTS - 2 and kind.startswith("stat"):
                                fold_stats(n[0] + TPB, t * 2 + par)
                pairs(dve, emit)
                for i in range(2):
                    dve_product(dve, 1, i)

        with nc.Block() as block:
            def pairs(eng, emit):
                emit("first", 0)
                with eng.Fori(1, TILES // 2 - 1) as t:
                    emit("pair", t)
                emit("last", TILES // 2 - 1)

            def tile(t, par):
                return (t * 2 + par, 1 - par, t)

            def order(v):
                def upto(first, last):
                    return max(0, min(COUPLES, (v - first + 1) * COUPLES // (last - first + 1)))

                def before(first, last):
                    return max(0, min(COUPLES, (v - first) * COUPLES // (last - first + 1)))
                ts = [("T", c) for c in range(before(1, 11), upto(1, 11))]
                cs = [("I", c) for c in range(before(2, 15), upto(2, 15))]
                both = []
                while ts or cs:
                    both += ts[:1] + cs[:1]
                    ts, cs = ts[1:], cs[1:]
                return both

            def done(what, v):
                return 1 + max([c for w in range(v + 1) for k, c in order(w) if k == what], default=-1)

            @block.sync
            def _(sp):
                sp.dma_start(ident_sb[:], ident).then_inc(const_in, 16)
                sp.dma_start(gm[:], gmats).then_inc(const_in, 16)

                def load(n, u, par):
                    sp.dma_start(part(XA[par], u).rearrange("p a b -> p (a b)"),
                                 x1a[bass.ds(n, 1), u].rearrange("a p n -> (a p) n")).then_inc(x_in[par][u], 16)
                    sp.dma_start(part(XB[par], u).rearrange("p a b -> p (a b)"),
                                 x1b[bass.ds(n, 1), u].rearrange("a p n -> (a p) n")).then_inc(x_in[par][u], 16)
                for u in range(PARTS):
                    load(0, u, 1)
                sp.wait_ge(w_low, 8)

                def store(n, g):
                    sp.wait_ge(o_taken, (n[0] - 1) * 32 + 4 * g + 4 + OBANK_AHEAD)
                    sp.dma_start(out[bass.ds(n[0] - 1, 1), g].rearrange("a p j n -> (a p) (j n)"),
                                 oring[:, g % 2].rearrange("p j n -> p (j n)")).then_inc(o_out[g % 2], 16)

                def stores(n, v):
                    for g in range(done("I", v - 1) // 4, done("I", v) // 4):
                        store(n, g)

                def emit(kind, t):
                    for par in range(2):
                        n = tile(t, par)
                        before = kind != "first" or par == 1
                        for v in range(UNITS):
                            if before:
                                for u in {0: (6,), 1: (7,)}.get(v, ()):
                                    load(n[0], u, n[1])
                                stores(n, v)
                            if v >= 11 and (kind != "last" or par == 0):
                                if before and v == 11:
                                    sp.wait_ge(t_ready, n[0] * 32)
                                for u in {11: (0, 1), 12: (2,), 13: (3,), 14: (4,), 15: (5,)}[v]:
                                    load(n[0] + 1, u, 1 - n[1])
                pairs(sp, emit)
                for v in range(UNITS):
                    stores((TILES, 0, TILES // 2), v)
                for s in range(2):
                    sp.wait_ge(o_out[s], TILES * PARTS // 2 * 16)

            @block.gpsimd
            def _(pool):
                pool.sem_inc(o_free, 2)
                with pool.Fori(0, TILES * PARTS // 2) as i:
                    for s in range(2):
                        pool.wait_ge(o_out[s], i * 16 + 16)
                        pool.sem_inc(o_free, 1)

            @block.scalar
            def _(act):
                act.sem_inc(t_taken, TBANK_AHEAD)
                act.sem_inc(o_taken, OBANK_AHEAD)
                act_weights(act, 1, (2,))
                act.wait_ge(s_dve, 3 * BATCH + 3)
                act.activation(work[:, 5, 0:8], work[:, 4, 0:8], ACT.Sqrt).then_inc(s_act, 1)
                act_weights(act, 1, (3,))

                def after(v, before):
                    c0 = before * COUPLES
                    for what, c in order(v):
                        if what == "T":
                            act.wait_ge(t_ready, c0 + c + 1)
                            act.wait_ge(inv_ready, c0 + c + 1 - TRING + INV_AHEAD)
                            act.copy(tring[:, c % TRING, :], psT[:, c % 2, 0:COUPLE]).then_inc(t_taken, 1)
                        else:
                            act.wait_ge(inv_ready, c0 + c + 1 + INV_AHEAD)
                            if c % 4 == 0:
                                act.wait_ge(o_free, before * PARTS + c // 4 + 1)
                            act.copy(oring[:, c // 4 % 2, c % 4, :], psO[c % 2]).then_inc(o_taken, 1)

                def emit(kind, t):
                    if kind == "first":
                        act.wait_ge(norm_ready, BATCH + 1)
                        act_high(act, tile(t, 0), 0, 1)
                    for par in range(2):
                        n = tile(t, par)
                        for u in range(PARTS):
                            for h in range(2):
                                if u + 1 < PARTS:
                                    act_high(act, n, u + 1, 1, "AB"[h])
                                elif kind != "last" or par == 0:
                                    act_high(act, tile(t + par, 1 - par), 0, 1, "AB"[h])
                                if kind != "first" or par == 1:
                                    after(2 * u + h, n[0] - 1)

                pairs(act, emit)
                for v in range(UNITS):
                    after(v, TILES - 1)

            @block.tensor
            def _(pe):
                pe.sem_inc(inv_ready, INV_AHEAD)
                pe.wait_ge(const_in, 16 * (CONSTS + 2))
                for i in range(2):
                    pe.wait_ge(s_dve, 3 * BATCH + 1 + i)
                    src = work[:, (0, 2)[i], 0:8]
                    for j in range(2):
                        pe.matmul(psS[:, BATCH * j:BATCH * (j + 1)], gm[:, 2 * j, :], src[:, 0:BATCH],
                                  start=True, stop=False)
                        mm = pe.matmul(psS[:, BATCH * j:BATCH * (j + 1)], gm[:, 2 * j + 1, :], src[:, BATCH:2 * BATCH],
                                       start=False, stop=True)
                    mm.then_inc(s_pe, 1)
                pe.wait_ge(s_dve, 3 * BATCH + 3)

                def after(v, n0, buf, ready):
                    for what, c in order(v):
                        if what == "T":
                            if c == 0:
                                pe.wait_ge(mix_taken, ready)
                            pe.wait_ge(t_taken, n0 * 32 + c - 1 + TBANK_AHEAD)
                            dst = psT[:, c % 2, :]
                            flatA = XA[buf][:].rearrange("p k n -> p (k n)")
                            flatB = XB[buf][:].rearrange("p k n -> p (k n)")
                            for e in range(2):
                                pe.transpose(dst[:, P * e:P * e + P], flatA[:, COUPLES * e + c::HALF], ident_sb[:])
                            pe.transpose(dst[:, 2 * P:3 * P], flatB[:, c::COUPLES], ident_sb[:]
                                         ).then_inc(t_ready, 1)
                        else:
                            pe.wait_ge(t_taken, n0 * 32 + c + 1 + TBANK_AHEAD)
                            pe.wait_ge(o_taken, n0 * 32 + c - 1 + OBANK_AHEAD)
                            pe.matmul(psO[c % 2], inv_sb[:], tring[:, c % TRING, :], start=True, stop=True
                                      ).then_inc(inv_ready, 1)

                def emit(kind, t):
                    for par in range(2):
                        n = tile(t, par)
                        for u in range(PARTS):
                            for h in range(2):
                                pe_mix(pe, n, u, TILES, (h,))
                                if kind != "first" or par == 1:
                                    after(2 * u + h, n[0] - 1, 1 - n[1], (n[0] + TILES) * 16 + EVAC_AHEAD)
                pairs(pe, emit)
                for v in range(UNITS):
                    after(v, TILES - 1, 0, 2 * TILES * 16 + EVAC_AHEAD)

            @block.vector
            def _(dve):
                k = Count()

                def link(ins):
                    ins.then_inc(step, 1)
                    dve.wait_ge(step, BATCH * LINKS0 + k.next())
                mean, var = work[:, 0, 0:8], work[:, 1, 0:8]
                mv = work[:, 8:10, 0:8].rearrange("p a b -> p (a b)").rearrange("p (r b m) -> p r b m", r=2, b=BATCH)
                sq = work[:, 10, 0:8]
                for r, (dc, sqs) in enumerate(((dcA, sqA), (dcB, sqB))):
                    for b in range(BATCH):
                        link(dve.bn_aggr(mv[:, r, b, :], dc[:, b * TPB * 6:(b + 1) * TPB * 6]))
                    link(dve.tensor_reduce(sq[:, BATCH * r:BATCH * (r + 1)],
                                           sqs[:].rearrange("p (b n) -> p b n", b=BATCH), AX.X, ALU.add))
                    link(dve.tensor_scalar(sq[:, BATCH * r:BATCH * (r + 1)], sq[:, BATCH * r:BATCH * (r + 1)],
                                           (1.0 + r) / POS, None, ALU.mult))
                mvf = mv.rearrange("p r b m -> p (r b) m")
                link(dve.tensor_scalar(mean, mvf[:, :, 0], 1.0 / PATCH, None, ALU.mult))
                link(dve.tensor_scalar(var, mvf[:, :, 1], 1.0 / SLOTS, None, ALU.mult))
                link(dve.tensor_tensor(var, var, sq, ALU.add))
                dve.sem_inc(s_dve, 1)
                dve_weight_low(dve, 1, 0)
                dve_product(dve, 1, 2)
                dve.wait_ge(s_pe, 2 * BATCH + 1)
                d = work[:, 3, 0:8]
                by_tile = "p r (b t) -> p (r b) t"
                link(dve.tensor_scalar(m1[:].rearrange(by_tile, b=BATCH),
                                       psS[:, 0:8].rearrange("p (n a) -> p n a", a=1).to_broadcast([P, 2 * BATCH, TPB]),
                                       -float(PATCH), None, ALU.mult))
                link(dve.tensor_tensor(d, mean, psS[:, 0:8], ALU.subtract))
                link(dve.tensor_tensor(d, d, d, ALU.mult))
                link(dve.tensor_tensor(work[:, 2, 0:8], d, var, ALU.add))
                dve.sem_inc(s_dve, 1)
                dve_weight_low(dve, 1, 1)
                dve.wait_ge(s_pe, 2 * BATCH + 2)
                dve_rstd(dve, link, psS[:, 0:8], 8, work[:, 11, 0:8], BATCH + 1,
                         lambda: dve_product(dve, 1, 3))
                link(dve.tensor_copy(r1[:].rearrange(by_tile, b=BATCH), work[:, 11, 0:8].rearrange("p (n a) -> p n a", a=1)
                                     .to_broadcast([P, 2 * BATCH, TPB])))
                assert k.n == LINKS1, k.n
                dve.sem_inc(norm_ready, 1)
                dve_weight_low(dve, 1, 2)
                dve_weight_low(dve, 1, 3)

                def emit(kind, t):
                    if kind == "first":
                        dve_low(dve, tile(t, 0), 0, 1)
                    for par in range(2):
                        n = tile(t, par)
                        for u in range(PARTS):
                            for h in range(2):
                                if u + 1 < PARTS:
                                    dve_low(dve, n, u + 1, 1, "AB"[h])
                                elif kind != "last" or par == 0:
                                    dve_low(dve, tile(t + par, 1 - par), 0, 1, "AB"[h])
                                dve_update(dve, n, u, h, 1, TILES)
                pairs(dve, emit)


def _constants():
    import numpy as np

    h, w = np.meshgrid(np.arange(PATCH), np.arange(PATCH), indexing="ij")
    rows = []
    for kh, kw in ((0, 0), (4, 0), (0, 4), (4, 4)):
        rows.append(np.cos(2 * np.pi * (kh * h + kw * w) / PATCH).ravel() / PATCH)
    pairs = [(kh, kw) for kh in range(PATCH) for kw in (1, 2, 3)] + [(kh, kw) for kw in (0, 4) for kh in (1, 2, 3)]
    for kh, kw in pairs:
        angle = 2 * np.pi * (kh * h + kw * w) / PATCH
        rows += [np.cos(angle).ravel() * 2 ** 0.5 / PATCH, np.sin(angle).ravel() * 2 ** 0.5 / PATCH]
    basis = np.array(rows)
    fwd = np.zeros((2, SLOTS, SLOTS, 2))
    for a in range(2):
        fwd[a, :, :, a] = basis.T
    fwd = fwd.reshape(P, P).astype(np.float32)
    c_a, c_b = np.arange(P), CA + np.arange(P) % CB
    def same(x, y, value):
        return np.where(x[:, None] // CPG == y[None, :] // CPG, value, 0.0)
    gmats = np.stack([same(c_a, c_a, 1 / CPG), same(c_b, c_a, 0.5 / CPG),
                      same(c_a, c_b, 1 / CPG), same(c_b, c_b, 0.5 / CPG)], axis=1).astype(np.float32)
    row_group = np.arange(P) // (P // GROUPS)
    def to(groups):
        return np.where(row_group[:, None] == groups[None, :], GROUPS / P, 0.0)
    smats = np.stack([to(row_group), to(c_a // CPG), to(c_b // CPG)], axis=1).astype(np.float32)
    return fwd, np.ascontiguousarray(fwd.T), np.eye(P, dtype=np.float32), gmats, smats


def kernel(x, L0_conv_w_proj, L0_conv_fft_filter, L1_conv_w_proj, L1_conv_fft_filter):
    import numpy as np
    import concourse.bacc as bacc
    from concourse.bass_utils import run_bass_kernel_spmd

    x = np.ascontiguousarray(x)
    v = x.reshape(BATCH, CH, TPB, 2, 2, PATCH, 4, 4, 2, PATCH)
    x_patch = np.ascontiguousarray(v.transpose(0, 2, 4, 6, 8, 5, 9, 3, 7, 1)).reshape(TILES, PARTS, P, NEWPAIRS, CH)
    fwd, inv, ident, gmats, smats = _constants()
    w0, w1 = np.ascontiguousarray(L0_conv_w_proj), np.ascontiguousarray(L1_conv_w_proj)
    arrays = {
        "x_stat": x.reshape(BATCH, P, XCOLS), "x_patch": x_patch,
        "w0": w0, "w1": w1, "wt0": np.ascontiguousarray(w0.T), "wt1": np.ascontiguousarray(w1.T),
        "f0": np.ascontiguousarray(L0_conv_fft_filter).reshape(CH, -1),
        "f1": np.ascontiguousarray(L1_conv_fft_filter).reshape(CH, -1),
        "fwd": fwd, "inv": inv, "ident": ident, "gmats": gmats, "smats": smats,
    }
    nc = bacc.Bacc("TRN2", target_bir_lowering=False, num_devices=1)
    args = [nc.dram_tensor(n, a.shape, mybir.dt.from_np(a.dtype), kind="ExternalInput").ap() for n, a in arrays.items()]
    out = nc.dram_tensor("out", (TILES, PARTS, P, 4, 2 * CH), F32, kind="ExternalOutput").ap()
    build(nc, *args, out)
    r = run_bass_kernel_spmd(nc, [arrays], core_ids=[0])
    got = r.results[0]["out"]
    got = got.reshape(BATCH, TPB, 4, 2, 2, PATCH, PATCH, 2, 2, 2 * CH)
    y = np.empty((BATCH, CH, TPB, 2, 2, PATCH, 4, 2, 2, 2, PATCH), got.dtype)
    y[:, :CA] = got[..., :2 * CA].reshape(*got.shape[:-1], 2, CA).transpose(0, 10, 1, 4, 9, 5, 2, 3, 7, 8, 6)
    y[:, CA:] = got[..., 2 * CA:].reshape(*got.shape[:-1], 2, CB).transpose(0, 10, 1, 9, 4, 5, 2, 3, 7, 8, 6)
    return y.reshape(BATCH, CH, HEIGHT, WIDTH)
```
